# Optimizing a Trainium2 kernel written in Bass

```python
import numpy as np
import jax
import jax.numpy as jnp

def _softmax(x, axis=-1):
    return jax.nn.softmax(x, axis=axis)

def _gelu(x):
    return jax.nn.gelu(x, approximate=True)

def _silu(x):
    return jax.nn.silu(x)

def _sigmoid(x):
    return jax.nn.sigmoid(x)

def _layernorm(x, axis=-1, eps=1e-05):
    m = jnp.mean(x, axis=axis, keepdims=True)
    v = jnp.var(x, axis=axis, keepdims=True)
    return (x - m) / jnp.sqrt(v + eps)

def _scatter_add(tgt, idx, src, axis=0):
    return tgt.at[idx].add(src)

def _segment_sum(src, seg, n):
    return jax.ops.segment_sum(src, seg, n)
kernel_name = 'mk_hybrid_d1_jaxref_r8_8eba8d'

def setup_inputs(seed: int=0):
    np.random.seed(seed)
    _w = jnp.asarray

    def _L0_attn_a_setup():
        import jax, jax.numpy as jnp
        import numpy as np
        HEADS = 16
        DIM_HEAD = 64
        EPS = 1e-08
        key = jax.random.key(seed)
        ks = jax.random.split(key, 5)
        B, N, D = (2, 256, 128)
        inner = HEADS * DIM_HEAD
        return {'x': jax.random.normal(ks[0], (B, N, D), jnp.float32), 'Wq': jax.random.normal(ks[1], (D, inner), jnp.float32) * D ** (-0.5), 'Wkv': jax.random.normal(ks[2], (D, 2 * inner), jnp.float32) * D ** (-0.5), 'Wo': jax.random.normal(ks[3], (inner, D), jnp.float32) * inner ** (-0.5), 'bo': jax.random.normal(ks[4], (D,), jnp.float32) * 0.02}
    _L0_attn_a_in = _L0_attn_a_setup()

    def _L0_attn_b_setup():
        import jax, jax.numpy as jnp
        import numpy as np
        N_HEADS = 16

        def _heads(x, h):
            B, T, D = x.shape
            return x.reshape(B, T, h, D // h).transpose(0, 2, 1, 3)

        def _reference_tuple_inner(x, Wq, Wk, Wv, Wo, Wg, bg):
            h = N_HEADS
            q = _heads(x @ Wq.T, h)
            k = _heads(x @ Wk.T, h)
            v = _heads(x @ Wv.T, h)
            g = _heads(jax.nn.sigmoid(x @ Wg.T + bg), h)
            qf = jax.nn.softplus(q) * (g + 1e-06)
            kf = jax.nn.softplus(k)
            kv = kf[..., :, None] * v[..., None, :]
            kv_cum = jnp.cumsum(kv, axis=2)
            z_cum = jnp.cumsum(kf, axis=2)
            num = jnp.einsum('bhtd,bhtde->bhte', qf, kv_cum)
            den = jnp.einsum('bhtd,bhtd->bht', qf, z_cum) + 1e-06
            out = num / den[..., None]
            B, _, T, dh = out.shape
            out = out.transpose(0, 2, 1, 3).reshape(B, T, h * dh)
            out = out @ Wo.T
            return (out, kv_cum[:, :, -1], z_cum[:, :, -1])
        key = jax.random.key(seed)
        B, T, D = (1, 256, 128)
        ks = jax.random.split(key, 7)
        s = 0.02
        return {'x': jax.random.normal(ks[0], (B, T, D), jnp.float32), 'Wq': jax.random.normal(ks[1], (D, D), jnp.float32) * s, 'Wk': jax.random.normal(ks[2], (D, D), jnp.float32) * s, 'Wv': jax.random.normal(ks[3], (D, D), jnp.float32) * s, 'Wo': jax.random.normal(ks[4], (D, D), jnp.float32) * s, 'Wg': jax.random.normal(ks[5], (D, D), jnp.float32) * s, 'bg': jax.random.normal(ks[6], (D,), jnp.float32) * s}
    _L0_attn_b_in = _L0_attn_b_setup()

    def _L0_ffn_setup():
        import jax, jax.numpy as jnp
        import numpy as np
        TOP_K = 2
        key = jax.random.key(seed)
        k1, k2, k3 = jax.random.split(key, 3)
        B, S, H, E, D = (4, 128, 128, 32, 128)
        x = jax.random.normal(k1, (B, S, H), dtype=jnp.float32)
        router_w = jax.random.normal(k2, (E, H), dtype=jnp.float32) * (1.0 / np.sqrt(H))
        bound = float(np.sqrt(6.0 / ((1.0 + 0.01 ** 2) * H)))
        expert_weights = jax.random.uniform(k3, (E, H, D), dtype=jnp.float32, minval=-bound, maxval=bound)
        return {'x': x, 'router_w': router_w, 'expert_weights': expert_weights}
    _L0_ffn_in = _L0_ffn_setup()
    _d = {'L0_attn_a_x': _L0_attn_a_in['x'], 'L0_attn_a_Wq': _L0_attn_a_in['Wq'], 'L0_attn_a_Wkv': _L0_attn_a_in['Wkv'], 'L0_attn_a_Wo': _L0_attn_a_in['Wo'], 'L0_attn_a_bo': _L0_attn_a_in['bo'], 'L0_attn_b_Wq': _L0_attn_b_in['Wq'], 'L0_attn_b_Wk': _L0_attn_b_in['Wk'], 'L0_attn_b_Wv': _L0_attn_b_in['Wv'], 'L0_attn_b_Wo': _L0_attn_b_in['Wo'], 'L0_attn_b_Wg': _L0_attn_b_in['Wg'], 'L0_attn_b_bg': _L0_attn_b_in['bg'], 'L0_ffn_router_w': _L0_ffn_in['router_w'], 'L0_ffn_expert_weights': _L0_ffn_in['expert_weights']}
    _x0 = _d['L0_attn_a_x']
    _d['L0_attn_a_x'] = jax.random.normal(jax.random.fold_in(jax.random.key(seed), 1), (4, 1024, 128), dtype=_x0.dtype)
    del _x0
    return _d

def reference(L0_attn_a_x, L0_attn_a_Wq, L0_attn_a_Wkv, L0_attn_a_Wo, L0_attn_a_bo, L0_attn_b_Wq, L0_attn_b_Wk, L0_attn_b_Wv, L0_attn_b_Wo, L0_attn_b_Wg, L0_attn_b_bg, L0_ffn_router_w, L0_ffn_expert_weights):

    def _L0_attn_a_ref(x, Wq, Wkv, Wo, bo):
        import jax, jax.numpy as jnp
        import numpy as np
        HEADS = 16
        DIM_HEAD = 64
        EPS = 1e-08
        B, N, D = x.shape
        H, Dh = (HEADS, DIM_HEAD)
        scale = Dh ** (-0.5)
        q = (x @ Wq).reshape(B, N, H, Dh).transpose(0, 2, 1, 3)
        kv = x @ Wkv
        k = kv[..., :H * Dh].reshape(B, N, H, Dh).transpose(0, 2, 1, 3)
        v = kv[..., H * Dh:].reshape(B, N, H, Dh).transpose(0, 2, 1, 3)
        s = jnp.einsum('bhid,bhjd->bhij', q * scale, k)
        gm = jax.lax.stop_gradient(jnp.max(s, axis=-1, keepdims=True))
        causal_mask = jnp.triu(jnp.ones((N, N), bool), 1)
        p = jnp.where(causal_mask, 0.0, jnp.exp(s - gm))
        num = jnp.einsum('bhij,bhjd->bhid', p, v)
        out = num / (jnp.sum(p, axis=-1, keepdims=True) + EPS)
        out = out.transpose(0, 2, 1, 3).reshape(B, N, H * Dh)
        return out @ Wo + bo

    def _L0_attn_b_ref(x, Wq, Wk, Wv, Wo, Wg, bg):
        import jax, jax.numpy as jnp
        import numpy as np
        N_HEADS = 16

        def _heads(x, h):
            B, T, D = x.shape
            return x.reshape(B, T, h, D // h).transpose(0, 2, 1, 3)

        def _reference_tuple_inner(x, Wq, Wk, Wv, Wo, Wg, bg):
            h = N_HEADS
            q = _heads(x @ Wq.T, h)
            k = _heads(x @ Wk.T, h)
            v = _heads(x @ Wv.T, h)
            g = _heads(jax.nn.sigmoid(x @ Wg.T + bg), h)
            qf = jax.nn.softplus(q) * (g + 1e-06)
            kf = jax.nn.softplus(k)
            kv = kf[..., :, None] * v[..., None, :]
            kv_cum = jnp.cumsum(kv, axis=2)
            z_cum = jnp.cumsum(kf, axis=2)
            num = jnp.einsum('bhtd,bhtde->bhte', qf, kv_cum)
            den = jnp.einsum('bhtd,bhtd->bht', qf, z_cum) + 1e-06
            out = num / den[..., None]
            B, _, T, dh = out.shape
            out = out.transpose(0, 2, 1, 3).reshape(B, T, h * dh)
            out = out @ Wo.T
            return (out, kv_cum[:, :, -1], z_cum[:, :, -1])
        return _reference_tuple_inner(x, Wq, Wk, Wv, Wo, Wg, bg)[0]

    def _L0_ffn_ref(x, router_w, expert_weights):
        import jax, jax.numpy as jnp
        import numpy as np
        TOP_K = 2
        B, S, H = x.shape
        E = router_w.shape[0]
        T = B * S
        logits = jnp.einsum('bsh,eh->bse', x, router_w)
        rw = jax.nn.softmax(logits, axis=-1).reshape(T, E)
        x_flat = x.reshape(T, H)
        vals, idx = jax.lax.top_k(rw, TOP_K)
        w_masked = jnp.zeros_like(rw).at[jnp.arange(T)[:, None], idx].set(vals)

        def body(acc, we):
            w_e, W_e = we
            return (acc + x_flat * w_e[:, None] @ W_e, None)
        out_flat, _ = jax.lax.scan(body, jnp.zeros((T, H), dtype=x.dtype), (w_masked.T, expert_weights))
        return out_flat.reshape(B, S, H)
    x = L0_attn_a_x
    x = x + _L0_attn_a_ref(_layernorm(x, axis=-1), L0_attn_a_Wq, L0_attn_a_Wkv, L0_attn_a_Wo, L0_attn_a_bo)
    x = x + _L0_ffn_ref(_layernorm(x, axis=-1), L0_ffn_router_w, L0_ffn_expert_weights)
    x = x + _L0_attn_b_ref(_layernorm(x, axis=-1), L0_attn_b_Wq, L0_attn_b_Wk, L0_attn_b_Wv, L0_attn_b_Wo, L0_attn_b_Wg, L0_attn_b_bg)
    x = x + _L0_ffn_ref(_layernorm(x, axis=-1), L0_ffn_router_w, L0_ffn_expert_weights)
    return x

_drawn_inputs = setup_inputs


def setup_inputs(seed=0):
    import zlib

    import numpy as np

    out = dict(_drawn_inputs(seed))
    spreads = {}
    factors = {'L0_attn_b_Wq': 8.0,
     'L0_attn_b_Wk': 8.0,
     'L0_attn_b_Wv': 4.294,
     'L0_attn_b_Wo': 4.273,
     'L0_attn_b_Wg': 8.0,
     'L0_attn_b_bg': 47.01}
    for name, (base, spread) in spreads.items():
        noise = np.random.default_rng([zlib.crc32(name.encode()), seed]).standard_normal(out[name].shape)
        drawn = base * np.exp(spread * noise) if base else spread * noise
        out[name] = jnp.asarray(drawn.astype(out[name].dtype))
    for name, factor in factors.items():
        out[name] = (out[name] * factor).astype(out[name].dtype)
    return out
```

```python
import concourse.bass as bass
from concourse import mybir
from contextlib import ExitStack

F32 = mybir.dt.float32
F32R = mybir.dt.float32r
ACT = mybir.ActivationFunctionType
ALU = mybir.AluOpType
AX = mybir.AxisListType

P = 128
B, N, D = 4, 1024, 128
T = B * N
CHUNKS = T // P
GROUP = 4
GROUPS = CHUNKS // GROUP
GT = GROUP * P
LN_EPS = 1e-5


def f(ap):
    return ap.bitcast(F32)


class Count:

    def __init__(self, engine, sem, value):
        self.engine, self.sem = engine, sem
        self.reg = engine.alloc_register(f"count_of_{sem.name}")
        engine.reg_mov(self.reg, value)

    def wait(self, more):
        self.engine.reg_add(self.reg, self.reg, more)
        self.engine.wait_ge(self.sem, self.reg)


class Scope:

    def __init__(self, nc, stack, phase):
        self.nc, self.stack, self.phase = nc, stack, phase

    def sb(self, name, shape, dt=F32):
        return self.stack.enter_context(self.nc.sbuf_tensor(f"{self.phase}_{name}", shape, dt))

    def ps(self, name, shape=(P, 512), dt=F32):
        return self.stack.enter_context(self.nc.psum_tensor(f"{self.phase}_{name}", list(shape), dt))

    def sem(self, name):
        return self.stack.enter_context(self.nc.semaphore(f"{self.phase}_{name}"))

    def block(self):
        return self.stack.enter_context(self.nc.Block())


def load_constants(nc, k, x_dram):
    with ExitStack() as stack:
        s = Scope(nc, stack, "consts")
        zeroed, made, x_in = s.sem("zeroed"), s.sem("made"), s.sem("x_in")
        block = s.block()

        @block.gpsimd
        def _(pool):
            pool.memset(k.ident[:, :], 0.0).then_inc(zeroed, 1)
            pool.wait_ge(zeroed, 1)
            pool.affine_select(out=k.ident[:, :], in_=k.ident[:, :], compare_op=ALU.not_equal, fill=1.0,
                               base=0, pattern=[[-1, P]], channel_multiplier=1).then_inc(made, 1)
            pool.memset(k.eps[:, :], LN_EPS).then_inc(made, 1)
            pool.wait_ge(made, 2)

        @block.sync
        def _(sync):
            for b in range(B):
                sync.dma_start(k.x[:, b * 8:(b + 1) * 8, :],
                               x_dram[b].rearrange("(c p) d -> p c d", p=P)).then_inc(x_in, 16)
            sync.wait_ge(x_in, 16 * B)


def normalise(nc, k, phase, router_w=None):
    E = 32
    with ExitStack() as stack:
        s = Scope(nc, stack, phase)
        stats = s.sb("stats", [P, CHUNKS, 6])
        mean, diff, var, std, rstd, shift = (s.sb(n, [P, CHUNKS]) for n in
                                             ("mean", "diff", "var", "std", "rstd", "shift"))
        xn = [s.sb(f"xn{i}", [P, GROUP, D]) for i in range(2)]
        hi = [s.sb(f"hi{i}", [P, GT], F32R) for i in range(2)]
        lo = [s.sb(f"lo{i}", [P, GT], F32R) for i in range(2)]
        turned = [s.ps(f"turned{i}") for i in range(2)]
        stats_ok, chain, std_ok, norm_ok, turn_ok = (s.sem(n) for n in ("stats_ok", "chain", "std_ok", "norm_ok", "turn_ok"))
        hi_ok, lo_ok = s.sem("hi_ok"), s.sem("lo_ok")
        kept = [s.sem(f"kept{i}") for i in range(2)]
        if router_w is not None:
            rw_raw = s.sb("rw_raw", [E, D])
            rT_hi, rT_lo = s.sb("rT_hi", [P, E], F32R), s.sb("rT_lo", [P, E], F32R)
            rT_ps = s.ps("rT_ps")
            logit_ps = [s.ps(f"logit_ps{i}") for i in range(2)]
            soft = [s.sb(f"soft{i}", [P, 16, E]) for i in range(2)]
            hot = [s.sb(f"hot{i}", [P, 16, E]) for i in range(2)]
            rest = [s.sb(f"rest{i}", [P, 16, E]) for i in range(2)]
            back = s.sb("back", [P, E])
            top, total = s.sb("top", [P, 2, 16]), s.sb("total", [P, 2, 16])
            rw_in, rw_turned, rw_hi_ok, rw_ok, logit_ok, exp_ok, back_ok, shifted = (s.sem(n) for n in (
                "rw_in", "rw_turned", "rw_hi_ok", "rw_ok", "logit_ok", "exp_ok", "back_ok", "shifted"))
        block = s.block()

        @block.sync
        def _(sync):
            if router_w is not None:
                sync.dma_start(rw_raw[:, :], router_w).then_inc(rw_in, 16)
            with sync.Fori(0, GROUPS // 2) as pair_of_groups:
                g = pair_of_groups * 2
                for i in range(2):
                    sync.wait_ge(hi_ok, g + (i + 1))
                    sync.wait_ge(lo_ok, g + (i + 1))
                    sync.dma_start(k.xT_hi[:, bass.ds(g * GT + i * GT, GT)], f(hi[i][:, :])).then_inc(kept[i], 16)
                    sync.dma_start(k.xT_lo[:, bass.ds(g * GT + i * GT, GT)], f(lo[i][:, :])).then_inc(kept[i], 16)
            for i in range(2):
                sync.wait_ge(kept[i], 32 * (GROUPS // 2))

        if router_w is not None:
            @block.gpsimd
            def _(pool):
                pool.iota(back[:, :], pattern=[[-1, E]], base=E, channel_multiplier=0,
                          allow_small_or_imprecise_dtypes=True).then_inc(back_ok, 1)

        @block.vector
        def _(dve):
            done = [0]

            def chained(ins):
                done[0] += 1
                ins.then_inc(chain, 1)
                dve.wait_ge(chain, done[0])

            with dve.Fori(0, CHUNKS) as c:
                dve.bn_stats(stats[:, bass.ds(c, 1), :].rearrange("p a s -> p (a s)"),
                             k.x[:, bass.ds(c, 1), :].rearrange("p a d -> p (a d)")).then_inc(stats_ok, 1)
            dve.wait_ge(stats_ok, CHUNKS)
            chained(dve.tensor_tensor(mean[:, :], stats[:, :, 1], stats[:, :, 4], ALU.add))
            chained(dve.tensor_tensor(diff[:, :], stats[:, :, 1], stats[:, :, 4], ALU.subtract))
            chained(dve.tensor_tensor(diff[:, :], diff[:, :], diff[:, :], ALU.mult))
            chained(dve.tensor_tensor(var[:, :], stats[:, :, 2], stats[:, :, 5], ALU.add))
            chained(dve.scalar_tensor_tensor(out=var[:, :], in0=diff[:, :], scalar=D / 4, in1=var[:, :],
                                             op0=ALU.mult, op1=ALU.add))
            dve.wait_ge(std_ok, 1)
            chained(dve.reciprocal(rstd[:, :], std[:, :]))
            chained(dve.scalar_tensor_tensor(out=shift[:, :], in0=mean[:, :], scalar=-0.5, in1=rstd[:, :],
                                             op0=ALU.mult, op1=ALU.mult))

            if router_w is not None:
                dve.wait_ge(rw_hi_ok, 1)
                dve.tensor_tensor(rT_lo[:, :], rT_ps[:, 0:E], f(rT_hi[:, :]), ALU.subtract).then_inc(rw_ok, 1)

            def norm(g, i):
                for c in range(GROUP):
                    at = bass.ds(g * GROUP + (i * GROUP + c), 1)
                    ins = dve.tensor_scalar(xn[i][:, c, :], k.x[:, at, :].rearrange("p a d -> p (a d)"),
                                            rstd[:, at], shift[:, at], ALU.mult, ALU.add)
                ins.then_inc(norm_ok, 1)

            def low(g, i):
                dve.wait_ge(hi_ok, g + (i + 1))
                dve.tensor_tensor(lo[i][:, :], turned[i][:, :], f(hi[i][:, :]), ALU.subtract).then_inc(lo_ok, 1)

            for i in range(2):
                norm(0, i)
            for i in range(2):
                low(0, i)
            with dve.Fori(1, GROUPS // 2) as pair_of_groups:
                g = pair_of_groups * 2
                for i in range(2):
                    dve.wait_ge(turn_ok, g + (i - 1))
                    norm(g, i)
                for i in range(2):
                    dve.wait_ge(kept[i], g * 16)
                    if router_w is not None:
                        dve.wait_ge(logit_ok, g + (i - 1))
                    low(g, i)

            if router_w is not None:
                dve.wait_ge(logit_ok, GROUPS)
                for i in range(2):
                    lg = logit_ps[i][:, :].rearrange("p (c e) -> p c e", e=E)
                    row = lambda a: a[:, i, :].unsqueeze(2).to_broadcast([P, 16, E])
                    chained(dve.tensor_reduce(top[:, i, :], lg, AX.X, ALU.max))
                    dve.tensor_tensor(soft[i][:, :, :], lg, row(top), ALU.subtract).then_inc(shifted, 1)
                for i in range(2):
                    row = lambda a: a[:, i, :].unsqueeze(2).to_broadcast([P, 16, E])
                    ids = back[:, :].unsqueeze(1).to_broadcast([P, 16, E])
                    dve.wait_ge(exp_ok, i + 1)
                    if i == 0:
                        dve.wait_ge(back_ok, 1)
                    chained(dve.tensor_reduce(total[:, i, :], soft[i][:, :, :], AX.X, ALU.add))
                    chained(dve.reciprocal(total[:, i, :], total[:, i, :]))
                    chained(dve.tensor_tensor(soft[i][:, :, :], soft[i][:, :, :], row(total), ALU.mult))
                    for rank in range(2):
                        have = soft[i] if rank == 0 else rest[i]
                        chained(dve.tensor_reduce(top[:, i, :], have[:, :, :], AX.X, ALU.max))
                        chained(dve.tensor_tensor(hot[i][:, :, :], have[:, :, :], row(top), ALU.is_equal))
                        chained(dve.tensor_tensor(hot[i][:, :, :], hot[i][:, :, :], ids, ALU.mult))
                        chained(dve.tensor_reduce(top[:, i, :], hot[i][:, :, :], AX.X, ALU.max))
                        chained(dve.tensor_tensor(hot[i][:, :, :], hot[i][:, :, :], row(top), ALU.is_equal))
                        if rank == 0:
                            chained(dve.scalar_tensor_tensor(out=rest[i][:, :, :], in0=hot[i][:, :, :], scalar=-4.0,
                                                             in1=soft[i][:, :, :], op0=ALU.mult, op1=ALU.add))
                            chained(dve.tensor_tensor(k.gate[i][:, :, :], hot[i][:, :, :], soft[i][:, :, :], ALU.mult))
                        else:
                            chained(dve.tensor_tensor(hot[i][:, :, :], hot[i][:, :, :], soft[i][:, :, :], ALU.mult))
                            chained(dve.tensor_tensor(k.gate[i][:, :, :], k.gate[i][:, :, :], hot[i][:, :, :], ALU.add))

        @block.scalar
        def _(act):
            act.wait_ge(chain, 5)
            act.activation(std[:, :], var[:, :], ACT.Sqrt, bias=k.eps[:, :], scale=1.0 / D).then_inc(std_ok, 1)
            if router_w is not None:
                act.wait_ge(rw_turned, 1)
                act.activation(rT_hi[:, :], rT_ps[:, 0:E], ACT.Copy).then_inc(rw_hi_ok, 1)

            def high(g, i):
                act.wait_ge(turn_ok, g + (i + 1))
                act.activation(hi[i][:, :], turned[i][:, :], ACT.Copy).then_inc(hi_ok, 1)

            for i in range(2):
                high(0, i)
            with act.Fori(1, GROUPS // 2) as pair_of_groups:
                g = pair_of_groups * 2
                for i in range(2):
                    act.wait_ge(kept[i], g * 16)
                    if router_w is not None:
                        act.wait_ge(logit_ok, g + (i - 1))
                    high(g, i)
            if router_w is not None:
                for i in range(2):
                    act.wait_ge(shifted, i + 1)
                    act.activation(soft[i][:, :, :], soft[i][:, :, :], ACT.Exp).then_inc(exp_ok, 1)

        @block.tensor
        def _(pe):
            if router_w is not None:
                pe.wait_ge(rw_in, 16)
                pe.transpose(rT_ps[:, 0:E], rw_raw[:, :], k.ident[0:E, 0:E]).then_inc(rw_turned, 1)

            def turn(g, i):
                pe.wait_ge(norm_ok, g + (i + 1))
                for c in range(GROUP):
                    ins = pe.transpose(turned[i][:, c * P:(c + 1) * P], xn[i][:, c, :], k.ident[:, :])
                ins.then_inc(turn_ok, 1)

            def route(g, i):
                pe.wait_ge(hi_ok, g + (i + 1))
                pe.wait_ge(lo_ok, g + (i + 1))
                for c in range(GROUP):
                    out = logit_ps[i][:, bass.ds(g * (GROUP * E // 2) + c * E, E)]
                    at = slice(c * P, (c + 1) * P)
                    pe.matmul(out, hi[i][:, at], rT_hi[:, :], start=True, stop=False)
                    pe.matmul(out, lo[i][:, at], rT_hi[:, :], start=False, stop=False)
                    ins = pe.matmul(out, hi[i][:, at], rT_lo[:, :], start=False, stop=True)
                ins.then_inc(logit_ok, 1)

            for i in range(2):
                turn(0, i)
            if router_w is not None:
                pe.wait_ge(rw_ok, 1)
            with pe.Fori(1, GROUPS // 2) as pair_of_groups:
                g = pair_of_groups * 2
                for i in range(2):
                    if router_w is not None:
                        route(g - 2, i)
                    pe.wait_ge(lo_ok, g + (i - 1))
                    turn(g, i)
            if router_w is not None:
                for i in range(2):
                    route(GROUPS - 2, i)


def experts(nc, k, phase, w_dram):
    E = 32
    PER = 4
    BANKS = 8
    QUADS = E // PER
    OPS = GROUP * QUADS
    PIECE = 8
    PRIMED = BANKS * PER + 2
    with ExitStack() as stack:
        s = Scope(nc, stack, phase)
        w_hi, w_lo = s.sb("w_hi", [P, E, D], F32R), s.sb("w_lo", [P, E, D], F32R)
        w_raw = s.sb("w_raw", [P, E, D])
        xs_hi = [s.sb(f"xs_hi{i}", [P, GT], F32R) for i in range(2)]
        xs_lo = [s.sb(f"xs_lo{i}", [P, GT], F32R) for i in range(2)]
        acc = [s.sb(f"acc{i}", [P, GROUP, D]) for i in range(2)]
        gate = [s.sb(f"gate{i}", [P, GROUP, E]) for i in range(2)]
        y = [s.ps(f"y{i}") for i in range(BANKS)]
        w_hi_ok, w_lo_ok, mm_ok, summed, acc_in, acc_out = (s.sem(n) for n in (
            "w_hi_ok", "w_lo_ok", "mm_ok", "summed", "acc_in", "acc_out"))
        w_in = [s.sem(f"w_in{q}") for q in range(E // PIECE)]
        xs_in = [s.sem(f"xs_in{i}") for i in range(2)]
        block = s.block()

        @block.sync
        def _(sync):
            for q in range(E // PIECE):
                sync.dma_start(w_raw[:, q * PIECE:(q + 1) * PIECE, :],
                               w_dram[q * PIECE:(q + 1) * PIECE].rearrange("e h d -> h e d")).then_inc(w_in[q], 16)

            def fetch(g, i):
                sync.dma_start(f(xs_hi[i][:, :]), k.xT_hi[:, bass.ds(g * GT + i * GT, GT)]).then_inc(xs_in[i], 16)
                sync.dma_start(f(xs_lo[i][:, :]), k.xT_lo[:, bass.ds(g * GT + i * GT, GT)]).then_inc(xs_in[i], 16)
            for i in range(2):
                fetch(0, i)
            with sync.Fori(1, GROUPS // 2) as pair_of_groups:
                g = pair_of_groups * 2
                for i in range(2):
                    sync.wait_ge(mm_ok, g * OPS + (i - 1) * OPS)
                    fetch(g, i)

        @block.gpsimd
        def _(pool):
            def begin(g, i):
                pool.tensor_copy(acc[i][:, :, :], k.x[:, bass.ds(g * GROUP + i * GROUP, GROUP), :]).then_inc(acc_in, 1)
                pool.tensor_copy(gate[i][:, :, :], k.gate[i][:, bass.ds(g * (GROUP // 2), GROUP), :]).then_inc(acc_in, 1)
            def end(g, i):
                pool.wait_ge(summed, g * (OPS * PER) + ((i + 1) * OPS * PER + PRIMED))
                pool.tensor_copy(k.x[:, bass.ds(g * GROUP + i * GROUP, GROUP), :], acc[i][:, :, :]).then_inc(acc_out, 1)
            for i in range(2):
                begin(0, i)
            with pool.Fori(1, GROUPS // 2) as pair_of_groups:
                g = pair_of_groups * 2
                for i in range(2):
                    end(g - 2, i)
                    pool.wait_ge(acc_out, g + (i - 1))
                    begin(g, i)
            for i in range(2):
                end(GROUPS - 2, i)
            pool.wait_ge(acc_out, GROUPS)

        @block.scalar
        def _(act):
            for q in range(E // PIECE):
                act.wait_ge(w_in[q], 16)
                at = slice(q * PIECE, (q + 1) * PIECE)
                act.activation(w_hi[:, at, :], w_raw[:, at, :], ACT.Copy).then_inc(w_hi_ok, 1)

        @block.vector
        def _(dve):
            dve.sem_inc(summed, PRIMED)
            for q in range(E // PIECE):
                dve.wait_ge(w_hi_ok, q + 1)
                at = slice(q * PIECE, (q + 1) * PIECE)
                dve.tensor_tensor(w_lo[:, at, :], w_raw[:, at, :], f(w_hi[:, at, :]), ALU.subtract).then_inc(w_lo_ok, 1)
            filled = Count(dve, mm_ok, 0)
            before = Count(dve, summed, PRIMED - 2)
            with dve.Fori(0, GROUPS // 2) as pair_of_groups:
                g = pair_of_groups * 2
                for i in range(2):
                    dve.wait_ge(acc_in, g * 2 + 2 * (i + 1))
                    for pair in range(GROUP // 2):
                        for quad in range(QUADS):
                            for e in range(PER):
                                for odd in range(2):
                                    if e == 0:
                                        filled.wait(1)
                                    before.wait(1)
                                    c = 2 * pair + odd
                                    n = quad * PER + e
                                    dve.scalar_tensor_tensor(
                                        out=acc[i][:, c, :], in0=y[(2 * quad + odd) % BANKS][:, e * D:(e + 1) * D],
                                        scalar=gate[i][:, c, n:n + 1], in1=acc[i][:, c, :],
                                        op0=ALU.mult, op1=ALU.add).then_inc(summed, 1)

        @block.tensor
        def _(pe):
            pe.wait_ge(w_lo_ok, E // PIECE)
            emptied = Count(pe, summed, PRIMED - BANKS * PER + 0)
            with pe.Fori(0, GROUPS // 2) as pair_of_groups:
                g = pair_of_groups * 2
                for i in range(2):
                    pe.wait_ge(xs_in[i], g * 16 + 32)
                    for pair in range(GROUP // 2):
                        for quad in range(QUADS):
                            for odd in range(2):
                                emptied.wait(1 if odd else 2 * PER - 1)
                                at = slice((2 * pair + odd) * P, (2 * pair + odd + 1) * P)
                                out = y[(2 * quad + odd) % BANKS][:, :]
                                hi = w_hi[:, quad * PER:(quad + 1) * PER, :].rearrange("h e d -> h (e d)")
                                lo = w_lo[:, quad * PER:(quad + 1) * PER, :].rearrange("h e d -> h (e d)")
                                pe.matmul(out, xs_hi[i][:, at], hi, start=True, stop=False)
                                pe.matmul(out, xs_hi[i][:, at], lo, start=False, stop=False)
                                pe.matmul(out, xs_lo[i][:, at], hi, start=False, stop=True).then_inc(mm_ok, 1)


class Rounds:

    def __init__(self, engine, sem, per, scratch):
        self.engine, self.sem, self.per, self.scratch = engine, sem, per, scratch
        self.fixed = -per
        self.base = engine.alloc_register(f"round_of_{sem.name}")
        engine.reg_mov(self.base, 0)

    def _wait(self, n):
        if self.fixed is not None:
            self.engine.wait_ge(self.sem, self.fixed + n)
        else:
            self.engine.reg_add(self.scratch, self.base, n)
            self.engine.wait_ge(self.sem, self.scratch)

    def now(self, n):
        self._wait(self.per + n + 1)

    def before(self, n):
        self._wait(n + 1)

    def enter_loop(self):
        self.fixed = None

    def forward(self):
        self.engine.reg_add(self.base, self.base, self.per)

    def leave_loop(self, rounds, not_done=0):
        self.fixed = rounds * self.per - not_done


def attention(nc, k, wq_dram, wkv_dram, wo_dram, bo_dram):
    H, DH = 16, 64
    PAIRS = H // 2
    ROUNDS = B * PAIRS
    BLOCKS = N // P
    SLOTS = 2 * BLOCKS
    HALF = 512
    SCALE = DH ** -0.5
    SUM_EPS = 1e-8
    MASKED = -1e30
    RING = 4
    SLOTS_WITH_UNIT = [*range(0, 4), *range(5, 16)]
    UNITS = len(SLOTS_WITH_UNIT)
    Q, K = 0, 1
    PLACE = {slot: n for n, slot in enumerate(SLOTS_WITH_UNIT)}
    SPLIT = {slot: n for n, slot in enumerate([0, 1, 2, 3, 5, 10, 11, 12, 13])}
    NOT_DONE = PLACE[5]
    PV_AT = {3: (0, 1, 1), 8: (1, 0, 0), 11: (2, 0, 1), 14: (3, 1, 0)}

    def turned_slot(s):
        t = (s - 2) % SLOTS
        return t // BLOCKS, t % BLOCKS

    with ExitStack() as stack:
        s_ = Scope(nc, stack, "attn")
        sb, ps, sem = s_.sb, s_.ps, s_.sem
        xs_hi, xs_lo = sb("xs_hi", [P, N], F32R), sb("xs_lo", [P, N], F32R)
        w_raw = sb("w_raw", [P, 2, H * DH])
        wv_hi, wv_lo = sb("wv_hi", [P, H * DH], F32R), sb("wv_lo", [P, H * DH], F32R)
        w_hi = [sb(f"w_hi{h}", [P, 2, 2, DH], F32R) for h in range(2)]
        w_lo = [sb(f"w_lo{h}", [P, 2, 2, DH], F32R) for h in range(2)]
        wo = sb("wo", [P, PAIRS, D])
        bo = sb("bo", [P, D])
        q_both = [sb(f"q_both{h}", [P, N], F32R) for h in range(2)]
        k_hi = [sb(f"k_hi{h}", [P, N], F32R) for h in range(2)]
        k_lo = [sb(f"k_lo{h}", [P, N], F32R) for h in range(2)]
        v = sb("v", [P, BLOCKS, 2, DH])
        v_next = sb("v_next", [P, BLOCKS, 2, DH])
        prob = [sb(f"prob{i}", [P, N]) for i in range(RING)]
        prob_t = [[sb(f"prob_t{h}{u}", [P, 4 * (u + 1), HALF]) for u in range(2)] for h in range(2)]
        o = sb("o", [P, N])
        o_norm = sb("o_norm", [P, N])
        neg_max = sb("neg_max", [P, RING])
        one = sb("one", [P, 1])
        row_sum, row_inv = sb("row_sum", [P, SLOTS]), sb("row_inv", [P, SLOTS])
        scale_hi, scale_lo = sb("scale_hi", [SLOTS, P], F32R), sb("scale_lo", [SLOTS, P], F32R)
        pick = sb("pick", [SLOTS, BLOCKS, P], F32R)
        pick_raw = sb("pick_raw", [SLOTS, BLOCKS, P])
        causal = sb("causal", [P, P])

        score = [ps(f"score{i}", (P, N)) for i in range(2)]
        turn = ps("turn", (P, N))
        pv = ps("pv")
        unit = ps("unit")

        s_ok, masked, exp_ok, turned, turn_out, pv_ok, o_ok, inv_ok, unit_ok, half_ok, unit_free, w_ok, v_ok = (
            sem(n) for n in ("s_ok", "masked", "exp_ok", "turned", "turn_out", "pv_ok", "o_ok", "inv_ok",
                             "unit_ok", "half_ok", "unit_free", "w_ok", "v_ok"))
        PER = {id(s_ok): 16, id(masked): 16, id(exp_ok): 16, id(turned): 16, id(turn_out): 16, id(v_ok): 1,
               id(pv_ok): 4, id(o_ok): 4, id(inv_ok): 2, id(unit_ok): UNITS, id(half_ok): len(SPLIT),
               id(unit_free): UNITS, id(w_ok): 4}
        wqk_in, wv_in, wo_in, bo_in, xs_in = (sem(n) for n in ("wqk_in", "wv_in", "wo_in", "bo_in", "xs_in"))
        scaled, wv_hi_ok, wv_ok, consts, primed, w_half, zeroed, maxed, summed, biased = (sem(n) for n in (
            "scaled", "wv_hi_ok", "wv_ok", "consts", "primed", "w_half", "zeroed", "maxed", "summed", "biased"))
        block = s_.block()
        wv_raw = prob_t[0][1][:, 0:2, :].rearrange("p a b -> p (a b)")

        def rounds(engine, *sems):
            scratch = engine.alloc_register(f"wait_value_{engine.engine.name}")
            return [Rounds(engine, x, PER[id(x)], scratch) for x in sems]

        @block.sync
        def _(sync):
            sync.dma_start(w_raw[:, 0, :], wq_dram).then_inc(wqk_in, 16)
            sync.dma_start(w_raw[:, 1, :], wkv_dram[:, 0:H * DH]).then_inc(wqk_in, 16)
            sync.dma_start(wv_raw, wkv_dram[:, H * DH:2 * H * DH]).then_inc(wv_in, 16)
            sync.dma_start(f(xs_hi[:, :]), k.xT_hi[:, 0:N]).then_inc(xs_in, 16)
            sync.dma_start(f(xs_lo[:, :]), k.xT_lo[:, 0:N]).then_inc(xs_in, 16)
            sync.dma_start(bo[:, :], bo_dram.rearrange("(a n) -> a n", a=1).to_broadcast([P, D])).then_inc(bo_in, 16)
            sync.dma_start(wo[:, :, :], wo_dram.rearrange("(h p) n -> p h n", p=P)).then_inc(wo_in, 16)
            units, = rounds(sync, unit_ok)
            units.enter_loop()
            with sync.Fori(0, ROUNDS) as it:
                units.now(PLACE[3])
                at = (((it + 1) >> 3) & (B - 1)) * N
                sync.dma_start(f(xs_hi[:, :]), k.xT_hi[:, bass.ds(at, N)]).then_inc(xs_in, 16)
                sync.dma_start(f(xs_lo[:, :]), k.xT_lo[:, bass.ds(at, N)]).then_inc(xs_in, 16)
                units.forward()

        @block.gpsimd
        def _(pool):
            pool.sem_inc(v_ok, 1)
            halves = pool.alloc_register("w_half_count")
            pool.reg_mov(halves, 2)

            def prepare(h, pair):
                for m in (Q, K):
                    src = w_raw[:, m, bass.ds(pair * (2 * DH) + h * DH, DH)].unsqueeze(1).to_broadcast([P, 2, DH])
                    pool.tensor_copy(w_hi[h][:, m, :, :], src).then_inc(w_half, 1)
                pool.wait_ge(w_half, halves)
                pool.reg_add(halves, halves, 2)
                for m in (Q, K):
                    src = w_raw[:, m, bass.ds(pair * (2 * DH) + h * DH, DH)].unsqueeze(1).to_broadcast([P, 2, DH])
                    pool.tensor_tensor(w_lo[h][:, m, :, :], src, f(w_hi[h][:, m, :, :]), ALU.subtract).then_inc(w_ok, 1)

            pool.memset(causal[:, :], 0.0).then_inc(zeroed, 1)
            pool.memset(pick_raw[:, :, :], 0.0).then_inc(zeroed, 1)
            pool.wait_ge(scaled, 1)
            pool.wait_ge(wqk_in, 32)
            prepare(0, 0)
            prepare(1, 0)
            pool.wait_ge(zeroed, 2)
            pool.affine_select(out=causal[:, :], in_=causal[:, :], compare_op=ALU.is_ge, fill=MASKED, base=0,
                               pattern=[[-1, P]], channel_multiplier=1).then_inc(consts, 1)
            pool.affine_select(out=pick_raw[:, :, :].rearrange("k b (h m) -> k b h m", h=2),
                               in_=pick_raw[:, :, :].rearrange("k b (h m) -> k b h m", h=2),
                               compare_op=ALU.not_equal, fill=1.0, base=0,
                               pattern=[[-1, BLOCKS], [-BLOCKS, 2], [0, DH]], channel_multiplier=1).then_inc(consts, 1)
            pool.wait_ge(consts, 2)
            pool.tensor_copy(pick[:, :, :], pick_raw[:, :, :]).then_inc(consts, 1)
            for t in (prob[2], o, o_norm, neg_max):
                pool.memset(t[:, :], 0.0).then_inc(primed, 1)
            pool.memset(prob_t[1][1][:, :, :], 0.0).then_inc(primed, 1)
            pool.memset(v[:, :, :, :], 0.0).then_inc(primed, 1)
            pool.memset(row_sum[:, :], 1.0).then_inc(primed, 1)
            pool.memset(row_inv[:, :], 1.0).then_inc(primed, 1)
            pool.memset(one[:, :], 1.0).then_inc(primed, 1)
            pool.wait_ge(primed, 10)
            pool.wait_ge(bo_in, 16)
            for b in range(B):
                xb = k.x[:, b * 8:(b + 1) * 8, :]
                pool.tensor_tensor(xb, xb, bo[:, :].unsqueeze(1).to_broadcast([P, 8, D]), ALU.add).then_inc(biased, 1)
            U, F, V = rounds(pool, unit_ok, unit_free, pv_ok)
            for r in (U, F, V):
                r.enter_loop()
            with pool.Fori(0, ROUNDS) as it:
                pair = (it + 1) & (PAIRS - 1)
                U.before(PLACE[13])
                prepare(0, pair)
                F.before(PLACE[15])
                V.now(0)
                flat = v_next[:, :, :, :].rearrange("p j h d -> p (j h d)")
                pool.tensor_tensor(v[:, :, :, :].rearrange("p j h d -> p (j h d)"), flat,
                                   one[:, :].to_broadcast([P, BLOCKS * 2 * DH]), ALU.mult).then_inc(v_ok, 1)
                U.now(PLACE[3])
                prepare(1, pair)
                for r in (U, F, V):
                    r.forward()

        @block.scalar
        def _(act):
            act.sem_inc(exp_ok, 16)
            act.sem_inc(turn_out, 16)
            act.sem_inc(o_ok, 4)
            act.sem_inc(half_ok, SPLIT[10])
            S, M, T, V, I, U, F, VC = rounds(act, s_ok, masked, turned, pv_ok, inv_ok, unit_ok, unit_free, v_ok)
            act.wait_ge(wqk_in, 32)
            act.activation(w_raw[:, Q, :], w_raw[:, Q, :], ACT.Copy, scale=SCALE).then_inc(scaled, 1)
            act.wait_ge(wv_in, 16)
            act.activation(wv_hi[:, :], wv_raw, ACT.Copy).then_inc(wv_hi_ok, 1)

            def copy_turned(s):
                h, b = turned_slot(s)
                T.now(s)
                if s in (2, 6, 10):
                    V.before({2: 1, 6: 2, 10: 3}[s])
                if s == 14:
                    V.now(0)
                n = b + 1
                act.activation(prob_t[h][b // 4][:, 0:n, (b % 4) * P:(b % 4 + 1) * P],
                               turn[:, 0:n * P].rearrange("p (j i) -> p j i", j=n), ACT.Copy).then_inc(turn_out, 1)

            def exponentials(slot):
                s = (slot - 1) % SLOTS
                b = s % BLOCKS
                M.now(s) if slot else M.before(s)
                T.now(slot - 3) if slot >= 3 else T.before(slot + 13)
                if s in (0, 8):
                    I.before(1) if s == 0 else I.now(0)
                w = (b + 1) * P
                act.activation(prob[s % RING][:, 0:w], score[s % 2][:, 0:w], ACT.Exp,
                               bias=neg_max[:, s % RING:s % RING + 1],
                               accum_out=row_sum[:, s:s + 1]).then_inc(exp_ok, 1)

            def unit_out(u, first=False):
                U.now(PLACE[u])
                if u < 4 or 10 <= u < 14:
                    h, m, half = int(u < 4), (u - 10 if u >= 10 else u) // 2, u % 2
                    if not first:
                        S.before(15) if u < 4 else S.now(7)
                    at = slice(half * HALF, (half + 1) * HALF)
                    act.activation((q_both if m == Q else k_hi)[h][:, at], unit[:, :], ACT.Copy).then_inc(half_ok, 1)
                elif u in (14, 15):
                    if not first:
                        VC.now(0)
                    at = slice((u - 14) * 4, (u - 13) * 4)
                    act.activation(v_next[:, at, :, :].rearrange("p j h d -> p (j h d)"), unit[:, :],
                                   ACT.Copy).then_inc(unit_free, 1)
                elif u == 5:
                    act.activation(scale_hi[:, :], unit[0:SLOTS, 0:P], ACT.Copy).then_inc(half_ok, 1)

            def product_out(s):
                n, h, half = PV_AT[s]
                V.now(n)
                if s in (8, 11):
                    F.now(PLACE[6 if s == 8 else 7])
                at = slice(half * HALF, (half + 1) * HALF)
                act.activation(o[h * DH:(h + 1) * DH, at], pv[h * DH:(h + 1) * DH, :], ACT.Copy).then_inc(o_ok, 1)

            def forward():
                for r in (S, M, T, V, I, U, F, VC):
                    r.forward()

            for u in range(10, 16):
                unit_out(u, first=True)
            for r in (S, M, T, V, I, U, F, VC):
                r.enter_loop()
            act.wait_ge(primed, 10)
            with act.Fori(0, ROUNDS) as _:
                for s in range(SLOTS):
                    if s in PLACE:
                        unit_out(s)
                    exponentials(s)
                    copy_turned(s)
                    if s in PV_AT:
                        product_out(s)
                forward()
            for r in (M, T, V, F):
                r.leave_loop(ROUNDS)
            U.leave_loop(ROUNDS, NOT_DONE)
            exponentials(0)
            copy_turned(0)
            copy_turned(1)
            product_out(3)
            unit_out(5)

        @block.vector
        def _(dve):
            dve.sem_inc(masked, 16)
            dve.sem_inc(inv_ok, 2)
            dve.sem_inc(unit_free, PLACE[10])
            S, E, O, U, HF, F = rounds(dve, s_ok, exp_ok, o_ok, unit_ok, half_ok, unit_free)
            dve.memset(score[1][:, :], 0.0).then_inc(primed, 1)
            dve.wait_ge(wv_hi_ok, 1)
            dve.tensor_tensor(wv_lo[:, :], wv_raw, f(wv_hi[:, :]), ALU.subtract).then_inc(wv_ok, 1)
            max_count, sum_count = dve.alloc_register("max_count"), dve.alloc_register("sum_count")
            dve.reg_mov(max_count, 0)
            dve.reg_mov(sum_count, 0)

            def maxima(s):
                b = s % BLOCKS
                S.now(s)
                dve.tensor_reduce(neg_max[:, s % RING:s % RING + 1], score[s % 2][:, :], AX.X, ALU.max,
                                  negate=True).then_inc(maxed, 1)
                dve.reg_add(max_count, max_count, 1)
                dve.wait_ge(maxed, max_count)
                diag = score[s % 2][:, b * P:(b + 1) * P]
                dve.tensor_tensor(diag, diag, causal[:, :], ALU.add).then_inc(masked, 1)

            def inverses(h):
                E.now(0) if h else E.now(8)
                if not h:
                    U.now(PLACE[5])
                cols = slice(h * BLOCKS, (h + 1) * BLOCKS)
                dve.tensor_scalar(row_sum[:, cols], row_sum[:, cols], SUM_EPS, None, ALU.add).then_inc(summed, 1)
                dve.reg_add(sum_count, sum_count, 1)
                dve.wait_ge(summed, sum_count)
                dve.reciprocal(row_inv[:, cols], row_sum[:, cols]).then_inc(inv_ok, 1)

            def unit_out(u, round_before=None):
                if u in SPLIT:
                    HF.now(SPLIT[u])
                if u < 4 or 10 <= u < 14:
                    h, m, half = int(u < 4), (u - 10 if u >= 10 else u) // 2, u % 2
                    at = slice(half * HALF, (half + 1) * HALF)
                    if m == Q:
                        rest = q_both[h][DH:P, at]
                        dve.tensor_tensor(rest, unit[DH:P, :], f(rest), ALU.subtract).then_inc(unit_free, 1)
                    else:
                        dve.tensor_tensor(k_lo[h][:, at], unit[:, :], f(k_hi[h][:, at]), ALU.subtract).then_inc(unit_free, 1)
                elif u == 5:
                    dve.tensor_tensor(scale_lo[:, :], unit[0:SLOTS, 0:P], f(scale_hi[:, :]), ALU.subtract).then_inc(unit_free, 1)
                elif u in (6, 7):
                    U.now(PLACE[u])
                    O.before(3) if u == 6 else O.now(0)
                    at = slice((u - 6) * HALF, (u - 5) * HALF)
                    dve.tensor_tensor(o_norm[:, at], unit[:, :], o[:, at], ALU.mult).then_inc(unit_free, 1)
                elif u in (8, 9):
                    U.now(PLACE[u])
                    F.before(PLACE[u])
                    x = k.x[:, bass.ds(((round_before >> 3) & (B - 1)) * 8 + (u - 8) * 4, 4), :]
                    dve.tensor_tensor(x, unit[:, :].rearrange("p (c d) -> p c d", d=D), x, ALU.add).then_inc(unit_free, 1)

            def forward():
                for r in (S, E, O, U, HF, F):
                    r.forward()

            for u in range(10, 14):
                unit_out(u)
            for r in (S, E, O, U, HF, F):
                r.enter_loop()
            dve.wait_ge(primed, 10)
            dve.wait_ge(consts, 3)
            dve.wait_ge(biased, B)
            with dve.Fori(0, ROUNDS) as it:
                for s in range(SLOTS):
                    if s in PLACE:
                        unit_out(s, (it + (ROUNDS - 1)) & (ROUNDS - 1))
                    maxima(s)
                    if s in (1, 9):
                        inverses(int(s == 1))
                forward()
            for r in (E, O, F):
                r.leave_loop(ROUNDS)
            U.leave_loop(ROUNDS, NOT_DONE)
            HF.leave_loop(ROUNDS, SPLIT[5])
            inverses(1)
            for u in range(5, 10):
                unit_out(u, ROUNDS - 1)

        @block.tensor
        def _(pe):
            pe.sem_inc(s_ok, 16)
            pe.sem_inc(turned, 16)
            pe.sem_inc(pv_ok, 4)
            pe.sem_inc(unit_ok, PLACE[10])
            E, TO, O, I, F, W, VC = rounds(pe, exp_ok, turn_out, o_ok, inv_ok, unit_free, w_ok, v_ok)
            xs_count = pe.alloc_register("xs_count")
            pe.reg_mov(xs_count, 32)

            def scores(s):
                h, b = s // BLOCKS, s % BLOCKS
                if b == 0:
                    F.now(PLACE[3]) if h else F.before(PLACE[13])
                E.now(s - 1) if s else E.before(15)
                q = q_both[h][:, b * P:(b + 1) * P]
                for half in range(2):
                    at = slice(half * HALF, (half + 1) * HALF)
                    pe.matmul(score[s % 2][:, at], q, k_hi[h][:, at], start=True, stop=False)
                    ins = pe.matmul(score[s % 2][:, at], q, k_lo[h][:, at], start=False, stop=True)
                ins.then_inc(s_ok, 1)

            def turn_round(s):
                h, b = turned_slot(s)
                E.now(s - 1) if s else E.before(15)
                TO.now(s - 1) if s else TO.before(15)
                src = prob[(s - 2) % RING]
                for j in range(b + 1):
                    ins = pe.transpose(turn[:, j * P:(j + 1) * P], src[:, j * P:(j + 1) * P], k.ident[:, :])
                ins.then_inc(turned, 1)

            def product(s):
                n, h, half = PV_AT[s]
                if s == 3:
                    VC.before(0)
                elif s == 8:
                    VC.now(0)
                TO.now({3: 1, 8: 5, 11: 9, 14: 13}[s])
                O.now(n - 1) if n else O.before(3)
                rows = slice(h * DH, (h + 1) * DH)
                for j in range(4 * (half + 1)):
                    at = slice(max(0, j * P - half * HALF), HALF)
                    ins = pe.matmul(pv[rows, at], v[:, j, h, :], prob_t[h][half][:, j, at],
                                    start=(j == 0), stop=(j == 4 * half + 3))
                ins.then_inc(pv_ok, 1)

            def one_unit(u, pair=None, first=False):
                if not first or u not in (5, 10):
                    F.now(PLACE[u] - 1) if u else F.before(UNITS - 1)
                if u < 4 or 10 <= u < 14:
                    h, m, half = int(u < 4), (u - 10 if u >= 10 else u) // 2, u % 2
                    if u == 0:
                        W.before(3)
                    if u == 10:
                        W.before(1) if first else W.now(1)
                        pe.wait_ge(xs_in, xs_count)
                        pe.reg_add(xs_count, xs_count, 32)
                    at = slice(half * HALF, (half + 1) * HALF)
                    hi = w_hi[h][:, m, :, :].rearrange("p a d -> p (a d)")
                    lo = w_lo[h][:, m, :, :].rearrange("p a d -> p (a d)")
                    pe.matmul(unit[:, :], hi, xs_hi[:, at], start=True, stop=False)
                    pe.matmul(unit[:, :], hi, xs_lo[:, at], start=False, stop=False)
                    ins = pe.matmul(unit[:, :], lo, xs_hi[:, at], start=False, stop=True)
                elif u in (14, 15):
                    cols = bass.ds(pair * (2 * DH), 2 * DH)
                    for j in range(4):
                        out = unit[:, j * P:(j + 1) * P]
                        rows = slice(((u - 14) * 4 + j) * P, ((u - 14) * 4 + j + 1) * P)
                        pe.matmul(out, xs_hi[:, rows], wv_hi[:, cols], start=True, stop=False)
                        pe.matmul(out, xs_lo[:, rows], wv_hi[:, cols], start=False, stop=False)
                        ins = pe.matmul(out, xs_hi[:, rows], wv_lo[:, cols], start=False, stop=True)
                elif u == 5:
                    I.now(0)
                    ins = pe.transpose(unit[0:SLOTS, 0:P], row_inv[:, :], k.ident[:, :])
                elif u in (6, 7):
                    for b in range(4):
                        out = unit[:, b * P:(b + 1) * P]
                        which = pick[:, (u - 6) * 4 + b, :]
                        pe.matmul(out, which, scale_hi[:, :], start=True, stop=False)
                        ins = pe.matmul(out, which, scale_lo[:, :], start=False, stop=True)
                else:
                    for b in range(4):
                        rows = slice(((u - 8) * 4 + b) * P, ((u - 8) * 4 + b + 1) * P)
                        ins = pe.matmul(unit[:, b * P:(b + 1) * P], o_norm[:, rows],
                                        wo[:, bass.ds(pair, 1), :].rearrange("p a d -> p (a d)"), start=True, stop=True)
                ins.then_inc(unit_ok, 1)

            def forward():
                for r in (E, TO, O, I, F, W, VC):
                    r.forward()

            W.fixed = 0
            pe.wait_ge(wv_ok, 1)
            for u in range(10, 16):
                one_unit(u, 0, first=True)
            for r in (E, TO, O, I, F, W, VC):
                r.enter_loop()
            pe.wait_ge(primed, 10)
            pe.wait_ge(wo_in, 16)
            pe.wait_ge(consts, 3)
            with pe.Fori(0, ROUNDS) as it:
                for s in range(SLOTS):
                    if s in PLACE:
                        one_unit(s, (it + (1 if s >= 10 else PAIRS - 1)) & (PAIRS - 1))
                    scores(s)
                    turn_round(s)
                    if s in PV_AT:
                        product(s)
                forward()
            for r in (E, TO, O, I, F, VC):
                r.leave_loop(ROUNDS)
            turn_round(0)
            turn_round(1)
            product(3)
            F.before(UNITS - 1)
            F.leave_loop(ROUNDS, NOT_DONE)
            for u in range(5, 10):
                one_unit(u, PAIRS - 1, first=u == 5)


def linear_attention(nc, k, wq_dram, wk_dram, wv_dram, wo_dram, wg_dram, bg_dram):
    HEADS, DH = 16, 8
    GATE_EPS, DEN_EPS = 1e-6, 1e-6
    HALVES = N // GT
    ROUNDS = B
    LEAD = 2
    COLS = DH + 1
    RING = 4
    WEIGHTS = 5
    WQ, WK, WG, WV, WO = range(WEIGHTS)
    ZQ, ZK, ZG = (slice(n * GT, (n + 1) * GT) for n in range(3))
    SUM_ORDER = [1, 2, 3, 0, 4, 5, 6, 7, 8]
    SUM_AT = {j: n for n, j in enumerate(SUM_ORDER)}

    with ExitStack() as stack:
        s_ = Scope(nc, stack, "linear")
        sb, ps, sem = s_.sb, s_.ps, s_.sem
        two = range(2)
        w = sb("w", [P, WEIGHTS, D])
        wT_hi, wT_lo = sb("wT_hi", [P, 3, D], F32R), sb("wT_lo", [P, 3, D], F32R)
        wv_hi, wv_lo = sb("wv_hi", [P, DH, HEADS, DH], F32R), sb("wv_lo", [P, DH, HEADS, DH], F32R)
        woT = sb("woT", [P, D])
        bg, ones = sb("bg", [P, 1]), sb("ones", [P, GT])
        same_head = sb("same_head", [P, HEADS, DH])
        into = sb("into", [P, DH, HEADS, DH])
        xs_hi = [sb(f"xs_hi{i}", [P, GT], F32R) for i in two]
        xs_lo = [sb(f"xs_lo{i}", [P, GT], F32R) for i in two]
        log = sb("log", [P, 2 * GT])
        gate, soft_q = sb("gate", [P, GT]), sb("soft_q", [P, GT])
        q, kk = ([sb(f"{n}{i}", [P, GT]) for i in two] for n in ("q", "k"))
        v_col = [sb(f"v_col{i}", [P, GT]) for i in two]
        kv_dve, kv_pool = ([sb(f"{n}{i}", [P, GT]) for i in two] for n in ("kv_dve", "kv_pool"))
        cum = [[sb(f"cum{i}_{j}", [P, GT]) for j in range(COLS)] for i in two]
        prod0 = [sb(f"prod0_{i}", [P, GT]) for i in two]
        prod = [sb(f"prod{i}", [P, GT]) for i in range(RING)]
        den_inv, oT = ([sb(f"{n}{i}", [P, GT]) for i in two] for n in ("den_inv", "oT"))
        z = ps("z", (P, 3 * GT))
        v_ps = [ps(f"v_ps{i}") for i in two]
        num = [ps(f"num{i}") for i in two]
        den_y = ps("den_y")

        w_in, bg_in, turned_ok, hi_ok, wT_ok, cleared, same_ok, const_ok = (sem(n) for n in (
            "w_in", "bg_in", "turned_ok", "hi_ok", "wT_ok", "cleared", "same_ok", "const_ok"))
        xs_in = [sem(f"xs_in{i}") for i in two]
        (z_ok, v_ok, v_out, kv_dve_ok, kv_pool_ok, cum_ok, prod_ok, sum_ok, gate_ok, log_step, soft_ok, q_ok,
         den_step, oT_ok, y_ok, x_ok) = (sem(n) for n in (
             "z_ok", "v_ok", "v_out", "kv_dve_ok", "kv_pool_ok", "cum_ok", "prod_ok", "sum_ok", "gate_ok", "log_step",
             "soft_ok", "q_ok", "den_step", "oT_ok", "y_ok", "x_ok"))
        PER = {id(x): n * HALVES for x, n in (
            (z_ok, 1), (v_ok, DH), (v_out, 4), (kv_dve_ok, 4), (kv_pool_ok, 4), (cum_ok, COLS), (prod_ok, COLS),
            (sum_ok, COLS), (gate_ok, 1), (log_step, 3), (soft_ok, 2), (q_ok, 1), (den_step, 2), (oT_ok, 1), (y_ok, 1), (x_ok, 1))}

        def rounds(engine, *sems):
            scratch = engine.alloc_register(f"linear_value_{engine.engine.name}")
            return [Rounds(engine, x, PER[id(x)], scratch) for x in sems]

        def at(r, g, n=0):
            m = g * (r.per // HALVES) + n
            r.now(m) if m >= 0 else r.before(m + r.per)

        def pipeline(slot, engine, sems):
            for x in sems:
                x.fixed = 0
            for n in range(LEAD):
                slot(n, 0)
            for x in sems:
                x.enter_loop()
            with engine.Fori(0, ROUNDS - 1) as r:
                for n in range(LEAD, LEAD + HALVES):
                    slot(n, r)
                for x in sems:
                    x.forward()
            for x in sems:
                x.fixed = (ROUNDS - 1) * x.per
            for n in range(LEAD, LEAD + HALVES):
                slot(n, ROUNDS - 1)

        def exists(g, r):
            return g >= 0 and not (isinstance(r, int) and r == ROUNDS - 1 and g >= HALVES)

        block = s_.block()

        @block.sync
        def _(sync):
            for n, d in enumerate((wq_dram, wk_dram, wg_dram, wv_dram, wo_dram)):
                sync.dma_start(w[:, n, :], d).then_inc(w_in, 16)
            sync.dma_start(bg[:, :], bg_dram.rearrange("(n a) -> n a", a=1)).then_inc(bg_in, 16)

            def fetch(g, i):
                sync.dma_start(f(xs_hi[i][:, :]), k.xT_hi[:, bass.ds(g * GT + i * GT, GT)]).then_inc(xs_in[i], 16)
                sync.dma_start(f(xs_lo[i][:, :]), k.xT_lo[:, bass.ds(g * GT + i * GT, GT)]).then_inc(xs_in[i], 16)
            V, = rounds(sync, v_ok)
            V.enter_loop()
            for i in two:
                fetch(0, i)
            with sync.Fori(1, ROUNDS) as r:
                for i in two:
                    at(V, i, DH - 1)
                    fetch(r * HALVES, i)
                V.forward()

        @block.gpsimd
        def _(pool):
            for x in (kv_pool_ok, prod_ok):
                pool.sem_inc(x, PER[id(x)])
            pool.memset(same_head[:, :, :], 1.0).then_inc(cleared, 1)
            pool.memset(into[:, :, :, :], 0.0).then_inc(cleared, 1)
            pool.memset(ones[:, :], 1.0).then_inc(const_ok, 1)
            pool.wait_ge(cleared, 2)
            pool.affine_select(out=same_head[:, :, :], in_=same_head[:, :, :], compare_op=ALU.is_ge, fill=0.0, base=0,
                               pattern=[[-DH, HEADS], [0, DH]], channel_multiplier=1).then_inc(same_ok, 1)
            pool.wait_ge(same_ok, 1)
            pool.affine_select(out=same_head[:, :, :], in_=same_head[:, :, :], compare_op=ALU.is_ge, fill=0.0,
                               base=DH - 1, pattern=[[DH, HEADS], [0, DH]], channel_multiplier=-1).then_inc(same_ok, 1)
            pool.wait_ge(same_ok, 2)
            for e in range(DH):
                pool.tensor_copy(into[:, e, :, e], same_head[:, :, e]).then_inc(const_ok, 1)
            V, C, S, SO, Q = waits = rounds(pool, v_out, cum_ok, sum_ok, soft_ok, q_ok)

            def slot(s, r):
                g = s - 1
                if not exists(g, r):
                    return
                i = g % 2

                def kv(j):
                    n = j // 2 - 1
                    if j == 2:
                        at(SO, g, 0)
                    at(V, g, n)
                    at(C, g, j - 4) if n >= 2 else at(C, g - 1, j + 4)
                    pool.tensor_tensor(kv_pool[n % 2][:, :], v_col[n % 2][:, :], kk[i][:, :], ALU.mult).then_inc(kv_pool_ok, 1)

                def product(j):
                    if j == 0:
                        at(Q, g)
                    at(C, g, j)
                    if j == 0:
                        at(S, g - 2, SUM_AT[0])
                    else:
                        at(S, g, SUM_AT[j - RING]) if j > RING else at(S, g - 1, SUM_AT[j + DH - RING])
                    out = prod0[i] if j == 0 else prod[(j - 1) % RING]
                    pool.tensor_tensor(out[:, :], q[i][:, :], cum[i][j][:, :], ALU.mult).then_inc(prod_ok, 1)

                kv(2)
                product(0)
                kv(4)
                product(1)
                product(2)
                kv(6)
                product(3)
                product(4)
                kv(8)
                for j in range(5, 9):
                    product(j)

            pipeline(slot, pool, waits)

        @block.scalar
        def _(act):
            for x in (v_out, gate_ok, log_step):
                act.sem_inc(x, PER[id(x)])
            act.wait_ge(turned_ok, 1)
            act.activation(wT_hi[:, :, :].rearrange("p a b -> p (a b)"), z[:, 0:3 * D], ACT.Copy).then_inc(hi_ok, 1)
            wvT = z[:, WV * D:(WV + 1) * D].rearrange("p (h e) -> p e h", h=HEADS).unsqueeze(3)
            act.activation(wv_hi[:, :, :, :], wvT.to_broadcast([P, DH, HEADS, DH]), ACT.Copy).then_inc(hi_ok, 1)
            act.activation(woT[:, :], z[:, WO * D:(WO + 1) * D], ACT.Copy).then_inc(hi_ok, 1)
            act.wait_ge(bg_in, 16)
            act.wait_ge(const_ok, 1 + DH)
            Z, V, L, SO, Q, KP = waits = rounds(act, z_ok, v_ok, log_step, soft_ok, q_ok, kv_pool_ok)

            def slot(s, r):
                g = s - 1

                def v_column(j):
                    if exists(g, r):
                        n = j // 2 - 1
                        at(V, g, j - 1)
                        at(KP, g, n - 2)
                        act.activation(v_col[n % 2][:, :], v_ps[j % 2][:, :], ACT.Copy).then_inc(v_out, 1)

                v_column(2)
                if exists(s, r):
                    at(Z, s)
                    at(Q, s - 1)
                    act.activation(gate[:, :], z[:, ZG], ACT.Sigmoid, bias=bg[:, :]).then_inc(gate_ok, 1)
                v_column(4)
                if exists(s, r):
                    at(SO, s - 1, 1)
                    act.activation(log[:, :], z[:, ZQ.start:ZK.stop], ACT.Abs).then_inc(log_step, 1)
                    at(L, s, 0)
                    act.activation(log[:, :], log[:, :], ACT.Exp, scale=-1.0).then_inc(log_step, 1)
                v_column(6)
                if exists(s, r):
                    at(L, s, 1)
                    act.activation(log[:, :], log[:, :], ACT.Ln, bias=ones[:, 0:1]).then_inc(log_step, 1)
                v_column(8)

            pipeline(slot, act, waits)

        @block.vector
        def _(dve):
            for x in (kv_dve_ok, cum_ok, soft_ok, q_ok, den_step, oT_ok, x_ok):
                dve.sem_inc(x, PER[id(x)])
            dve.wait_ge(hi_ok, 3)
            dve.tensor_tensor(wT_lo[:, :, :].rearrange("p a b -> p (a b)"), z[:, 0:3 * D],
                              f(wT_hi[:, :, :].rearrange("p a b -> p (a b)")), ALU.subtract).then_inc(wT_ok, 1)
            wvT = z[:, WV * D:(WV + 1) * D].rearrange("p (h e) -> p e h", h=HEADS).unsqueeze(3)
            dve.tensor_tensor(wv_lo[:, :, :, :], wvT.to_broadcast([P, DH, HEADS, DH]),
                              f(wv_hi[:, :, :, :]), ALU.subtract).then_inc(wT_ok, 1)
            dve.wait_ge(const_ok, 1 + DH)
            V, KD, KP, C, PR, SU, G, L, SO, DE, OT, Y = waits = rounds(
                dve, v_ok, kv_dve_ok, kv_pool_ok, cum_ok, prod_ok, sum_ok, gate_ok, log_step, soft_ok, den_step, oT_ok, y_ok)

            def slot(s, r):
                g, back = s - 1, s - 2
                i = g % 2

                def kv(j):
                    n = j // 2
                    if j == 1:
                        at(SO, g, 0)
                    at(V, g, j - 1)
                    at(C, g, j - 4) if n >= 2 else at(C, g - 1, j + 4)
                    dve.tensor_tensor(kv_dve[n % 2][:, :], v_ps[j % 2][:, :], kk[i][:, :], ALU.mult).then_inc(kv_dve_ok, 1)

                def scan(j):
                    if j == 0:
                        src = kk[i]
                    elif j % 2:
                        at(KD, g, j // 2)
                        src = kv_dve[j // 2 % 2]
                    else:
                        at(KP, g, j // 2 - 1)
                        src = kv_pool[(j // 2 - 1) % 2]
                    at(PR, g - 2, j)
                    at(C, g - 1, j)
                    start = cum[0][j][:, GT - 1:GT] if i else 0.0
                    dve.tensor_tensor_scan(cum[i][j][:, :], ones[:, :], src[:, :], start,
                                           ALU.mult, ALU.add).then_inc(cum_ok, 1)

                main, front, out = exists(g, r), exists(s, r), exists(back, r)
                if main:
                    kv(1)
                    scan(0)
                    kv(3)
                if out:
                    at(SU, back, COLS - 1)
                    at(DE, back, 1)
                    at(Y, back - 2)
                    dve.tensor_tensor(oT[back % 2][:, :], num[back % 2][:, :], den_inv[back % 2][:, :],
                                      ALU.mult).then_inc(oT_ok, 1)
                if main:
                    scan(1)
                    scan(2)
                    kv(5)
                if out:
                    at(Y, back)
                    x = k.x[:, bass.ds(r * (HALVES * GROUP) + back * GROUP, GROUP), :]
                    dve.tensor_tensor(x, den_y[:, :].rearrange("p (c d) -> p c d", d=D), x, ALU.add).then_inc(x_ok, 1)
                if main:
                    scan(3)
                    scan(4)
                    kv(7)
                    scan(5)
                    at(SU, g, SUM_AT[0])
                    at(OT, g - 2)
                    dve.tensor_scalar(den_inv[i][:, :], den_y[:, :], DEN_EPS, None, ALU.add).then_inc(den_step, 1)
                    scan(6)
                    at(DE, g, 0)
                    dve.reciprocal(den_inv[i][:, :], den_inv[i][:, :]).then_inc(den_step, 1)
                if front:
                    at(L, s, 2)
                    at(PR, s - 2, COLS - 1)
                    at(C, s - 2, 0)
                    dve.scalar_tensor_tensor(out=kk[s % 2][:, :], in0=z[:, ZK], scalar=0.0, in1=log[:, ZK],
                                             op0=ALU.max, op1=ALU.add).then_inc(soft_ok, 1)
                    dve.scalar_tensor_tensor(out=soft_q[:, :], in0=z[:, ZQ], scalar=0.0, in1=log[:, ZQ],
                                             op0=ALU.max, op1=ALU.add).then_inc(soft_ok, 1)
                if main:
                    scan(7)
                if front:
                    at(G, s)
                    at(SO, s, 1)
                    dve.scalar_tensor_tensor(out=q[s % 2][:, :], in0=gate[:, :], scalar=GATE_EPS, in1=soft_q[:, :],
                                             op0=ALU.add, op1=ALU.mult).then_inc(q_ok, 1)
                if main:
                    scan(8)

            pipeline(slot, dve, waits)

        @block.tensor
        def _(pe):
            for x in (z_ok, v_ok, sum_ok, y_ok):
                pe.sem_inc(x, PER[id(x)])
            pe.wait_ge(w_in, 16 * WEIGHTS)
            for n in range(WEIGHTS):
                ins = pe.transpose(z[:, n * D:(n + 1) * D], w[:, n, :], k.ident[:, :])
            ins.then_inc(turned_ok, 1)
            pe.wait_ge(wT_ok, 2)
            pe.wait_ge(const_ok, 1 + DH)
            KD, VO, PR, SO, G, OT, X, DE = waits = rounds(pe, kv_dve_ok, v_out, prod_ok, soft_ok, gate_ok, oT_ok, x_ok, den_step)
            xs_count, xs_value = pe.alloc_register("linear_xs_count"), pe.alloc_register("linear_xs_value")
            pe.reg_mov(xs_count, 0)

            def three(out, w_hi, w_lo, x_hi, x_lo):
                pe.matmul(out, w_hi, x_hi, start=True, stop=False)
                pe.matmul(out, w_hi, x_lo, start=False, stop=False)
                return pe.matmul(out, w_lo, x_hi, start=False, stop=True)

            def projections(g, r):
                i = g % 2
                if isinstance(r, int):
                    pe.wait_ge(xs_in[i], 32 * (r + g // 2 + 1))
                else:
                    pe.reg_add(xs_value, xs_count, 32 * (g // 2 + 1))
                    pe.wait_ge(xs_in[i], xs_value)
                at(SO, g - 1, 1)
                at(G, g - 1)
                for n, cols in ((WG, ZG), (WQ, ZQ), (WK, ZK)):
                    ins = three(z[:, cols], wT_hi[:, n, :], wT_lo[:, n, :], xs_hi[i][:, :], xs_lo[i][:, :])
                ins.then_inc(z_ok, 1)

            def v_column(g, j):
                if j % 2:
                    at(KD, g, j // 2 - 1)
                else:
                    at(VO, g, j // 2 - 2)
                hi, lo = (t[:, j - 1, :, :].rearrange("p h d -> p (h d)") for t in (wv_hi, wv_lo))
                three(v_ps[j % 2][:, :], hi, lo, xs_hi[g % 2][:, :], xs_lo[g % 2][:, :]).then_inc(v_ok, 1)

            def sum_over_d(g, j):
                at(PR, g, j)
                if j == 0:
                    at(X, g - 1)
                    pe.matmul(den_y[:, :], same_head[:, :, :].rearrange("p h d -> p (h d)"), prod0[g % 2][:, :],
                              start=True, stop=True).then_inc(sum_ok, 1)
                else:
                    if j == 1:
                        at(OT, g - 2)
                    pe.matmul(num[g % 2][:, :], into[:, j - 1, :, :].rearrange("p h d -> p (h d)"),
                              prod[(j - 1) % RING][:, :], start=(j == 1), stop=(j == DH)).then_inc(sum_ok, 1)

            def slot(s, r):
                g, back = s - 1, s - 2
                main, front, out = exists(g, r), exists(s, r), exists(back, r)
                if front:
                    projections(s, r)
                if main:
                    v_column(g, 3)
                    v_column(g, 4)
                if out:
                    at(OT, back)
                    at(DE, back, 0)
                    for c in range(GROUP):
                        at_c = slice(c * P, (c + 1) * P)
                        ins = pe.matmul(den_y[:, at_c], oT[back % 2][:, at_c], woT[:, :], start=True, stop=True)
                    ins.then_inc(y_ok, 1)
                if main:
                    v_column(g, 5)
                    sum_over_d(g, 1)
                    v_column(g, 6)
                    sum_over_d(g, 2)
                    v_column(g, 7)
                    sum_over_d(g, 3)
                    sum_over_d(g, 0)
                    v_column(g, 8)
                    sum_over_d(g, 4)
                if front:
                    v_column(s, 1)
                if main:
                    sum_over_d(g, 5)
                if front:
                    v_column(s, 2)
                if main:
                    sum_over_d(g, 6)
                    sum_over_d(g, 7)
                    sum_over_d(g, 8)
                if s == LEAD + HALVES - 1:
                    pe.reg_add(xs_count, xs_count, 32)

            pipeline(slot, pe, waits)


def store(nc, k, out_dram):
    with ExitStack() as stack:
        s = Scope(nc, stack, "store")
        stored = s.sem("stored")
        block = s.block()

        @block.sync
        def _(sync):
            for b in range(B):
                sync.dma_start(out_dram[b].rearrange("(c p) d -> p c d", p=P),
                               k.x[:, b * 8:(b + 1) * 8, :]).then_inc(stored, 16)
            sync.wait_ge(stored, 16 * B)


class Kept:
    pass


def network(nc, x, a_wq, a_wkv, a_wo, a_bo, b_wq, b_wk, b_wv, b_wo, b_wg, b_bg, router_w, expert_w, out):
    with ExitStack() as stack:
        s = Scope(nc, stack, "kept")
        k = Kept()
        k.x = s.sb("x", [P, CHUNKS, D])
        k.xT_hi, k.xT_lo = s.sb("xT_hi", [P, T]), s.sb("xT_lo", [P, T])
        k.gate = [s.sb(f"gate{i}", [P, 16, 32]) for i in range(2)]
        k.ident = s.sb("ident", [P, P])
        k.eps = s.sb("eps", [P, 1])
        load_constants(nc, k, x)
        if "A" in STAGES:
            normalise(nc, k, "norm_a")
            attention(nc, k, a_wq, a_wkv, a_wo, a_bo)
        if "F" in STAGES:
            normalise(nc, k, "norm_f1", router_w)
            experts(nc, k, "experts1", expert_w)
        if "B" in STAGES:
            normalise(nc, k, "norm_b")
            linear_attention(nc, k, b_wq, b_wk, b_wv, b_wo, b_wg, b_bg)
        if "G" in STAGES:
            normalise(nc, k, "norm_f2", router_w)
            experts(nc, k, "experts2", expert_w)
        store(nc, k, out)

STAGES = "AFBG"

_INS = ['L0_attn_a_x', 'L0_attn_a_Wq', 'L0_attn_a_Wkv', 'L0_attn_a_Wo', 'L0_attn_a_bo', 'L0_attn_b_Wq', 'L0_attn_b_Wk',
        'L0_attn_b_Wv', 'L0_attn_b_Wo', 'L0_attn_b_Wg', 'L0_attn_b_bg', 'L0_ffn_router_w', 'L0_ffn_expert_weights']
_OUTS = [((B, N, D), 'float32')]


def kernel(**inputs):
    import numpy as _np
    import concourse.bacc as _bacc
    from concourse import mybir as _mybir
    from concourse.bass_utils import run_bass_kernel_spmd as _run

    nc = _bacc.Bacc("TRN2", target_bir_lowering=False, num_devices=1)
    arrays, args = {}, []
    for name in _INS:
        a = _np.ascontiguousarray(inputs[name])
        arrays[f"in_{name}_dram"] = a
        args.append(nc.dram_tensor(f"in_{name}_dram", a.shape, _mybir.dt.from_np(a.dtype), kind="ExternalInput").ap())
    for i, (shape, dtype) in enumerate(_OUTS):
        dt = _mybir.dt.from_np(_np.dtype(dtype))
        args.append(nc.dram_tensor(f"out_{i}_dram", shape, dt, kind="ExternalOutput").ap())
    network(nc, *args)
    r = _run(nc, [arrays], core_ids=[0])
    got = tuple(r.results[0][f"out_{i}_dram"] for i in range(len(_OUTS)))
    return got[0]
```

```python
import concourse.bass as bass
from concourse import mybir
from contextlib import ExitStack

F32 = mybir.dt.float32
F32R = mybir.dt.float32r
ACT = mybir.ActivationFunctionType
ALU = mybir.AluOpType
AX = mybir.AxisListType

P = 128
B, N, D = 4, 1024, 128
T = B * N
CHUNKS = T // P
GROUP = 4
GROUPS = CHUNKS // GROUP
GT = GROUP * P
LN_EPS = 1e-5


def f(ap):
    return ap.bitcast(F32)


class Count:

    def __init__(self, engine, sem, value):
        self.engine, self.sem = engine, sem
        self.reg = engine.alloc_register(f"count_of_{sem.name}")
        engine.reg_mov(self.reg, value)

    def wait(self, more):
        self.engine.reg_add(self.reg, self.reg, more)
        self.engine.wait_ge(self.sem, self.reg)


class Scope:

    def __init__(self, nc, stack, phase):
        self.nc, self.stack, self.phase = nc, stack, phase

    def sb(self, name, shape, dt=F32):
        return self.stack.enter_context(self.nc.sbuf_tensor(f"{self.phase}_{name}", shape, dt))

    def ps(self, name, shape=(P, 512), dt=F32):
        return self.stack.enter_context(self.nc.psum_tensor(f"{self.phase}_{name}", list(shape), dt))

    def sem(self, name):
        return self.stack.enter_context(self.nc.semaphore(f"{self.phase}_{name}"))

    def block(self):
        return self.stack.enter_context(self.nc.Block())


def load_constants(nc, k, x_dram):
    with ExitStack() as stack:
        s = Scope(nc, stack, "consts")
        zeroed, made, x_in = s.sem("zeroed"), s.sem("made"), s.sem("x_in")
        block = s.block()

        @block.gpsimd
        def _(pool):
            pool.memset(k.ident[:, :], 0.0).then_inc(zeroed, 1)
            pool.wait_ge(zeroed, 1)
            pool.affine_select(out=k.ident[:, :], in_=k.ident[:, :], compare_op=ALU.not_equal, fill=1.0,
                               base=0, pattern=[[-1, P]], channel_multiplier=1).then_inc(made, 1)
            pool.memset(k.eps[:, :], LN_EPS).then_inc(made, 1)
            pool.wait_ge(made, 2)

        @block.sync
        def _(sync):
            for b in range(B):
                sync.dma_start(k.x[:, b * 8:(b + 1) * 8, :],
                               x_dram[b].rearrange("(c p) d -> p c d", p=P)).then_inc(x_in, 16)
            sync.wait_ge(x_in, 16 * B)


def normalise(nc, k, phase, router_w=None, expert_w=None):
    E = 32
    TOP = 8
    HALF = CHUNKS // 2
    UNROLL = 8
    PIECE = 8
    with ExitStack() as stack:
        s = Scope(nc, stack, phase)
        stats = s.sb("stats", [P, CHUNKS, 6])
        mean, diff, var, std, rstd, shift = (s.sb(n, [P, CHUNKS]) for n in
                                             ("mean", "diff", "var", "std", "rstd", "shift"))
        xn = [s.sb(f"xn{i}", [P, GROUP, D]) for i in range(2)]
        raw = [s.sb(f"raw{i}", [P, GT]) for i in range(2)]
        hi = [s.sb(f"hi{i}", [P, GT], F32R) for i in range(2)]
        lo = [s.sb(f"lo{i}", [P, GT], F32R) for i in range(2)]
        turned = [s.ps(f"turned{i}") for i in range(2)]
        stats_ok, chain, std_ok, norm_ok, turn_ok = (s.sem(n) for n in ("stats_ok", "chain", "std_ok", "norm_ok", "turn_ok"))
        hi_ok, lo_ok, raw_ok = s.sem("hi_ok"), s.sem("lo_ok"), s.sem("raw_ok")
        kept = [s.sem(f"kept{i}") for i in range(2)]
        if router_w is not None:
            rw_raw = s.sb("rw_raw", [E, D])
            rT = s.sb("rT", [P, 2, E], F32R)
            rT_ps = s.ps("rT_ps")
            logit = s.ps("logit", (P, CHUNKS * 2 * E))
            soft = [s.sb(f"soft{i}", [P, HALF, E + TOP]) for i in range(2)]
            rest = [s.sb(f"rest{i}", [P, HALF, E + TOP]) for i in range(2)]
            best = [s.sb(f"best{i}", [P, HALF, TOP]) for i in range(2)]
            top, total = s.sb("top", [P, 2, HALF]), s.sb("total", [P, 2, HALF])
            rw_in, rw_turned, rw_hi_ok, rw_ok, logit_ok, exp_ok, none_ok, shifted = (s.sem(n) for n in (
                "rw_in", "rw_turned", "rw_hi_ok", "rw_ok", "logit_ok", "exp_ok", "none_ok", "shifted"))
        if expert_w is not None:
            w_raw = s.sb("w_raw", [P, E, D])
            w_in = [s.sem(f"w_in{q}") for q in range(E // PIECE)]
            w_hi_ok, w_lo_ok = s.sem("w_hi_ok"), s.sem("w_lo_ok")
        block = s.block()
        NONE = -1.0

        @block.sync
        def _(sync):
            if router_w is not None:
                sync.dma_start(rw_raw[:, :], router_w).then_inc(rw_in, 16)
            if expert_w is not None:
                for q in range(E // PIECE):
                    sync.dma_start(w_raw[:, q * PIECE:(q + 1) * PIECE, :],
                                   expert_w[q * PIECE:(q + 1) * PIECE].rearrange("e h d -> h e d")).then_inc(w_in[q], 16)
            with sync.Fori(0, GROUPS // 2) as pair_of_groups:
                g = pair_of_groups * 2
                for i in range(2):
                    sync.wait_ge(lo_ok, g + (i + 1))
                    sync.dma_start(k.xT_hi[:, bass.ds(g * GT + i * GT, GT)], f(hi[i][:, :])).then_inc(kept[i], 16)
                    sync.dma_start(k.xT_lo[:, bass.ds(g * GT + i * GT, GT)], f(lo[i][:, :])).then_inc(kept[i], 16)
            for i in range(2):
                sync.wait_ge(kept[i], 32 * (GROUPS // 2))

        @block.gpsimd
        def _(pool):
            def split_experts(pieces):
                for q in pieces:
                    at = slice(q * PIECE, (q + 1) * PIECE)
                    pool.wait_ge(w_hi_ok, q + 1)
                    pool.tensor_tensor(k.w_lo[:, at, :], w_raw[:, at, :], f(k.w_hi[:, at, :]), ALU.subtract).then_inc(w_lo_ok, 1)

            if router_w is not None:
                for i in range(2):
                    pool.memset(soft[i][:, :, E:E + TOP], NONE).then_inc(none_ok, 1)

            def low(g, i):
                pool.wait_ge(raw_ok, g + (i + 1))
                pool.tensor_tensor(lo[i][:, :], raw[i][:, :], f(hi[i][:, :]), ALU.subtract).then_inc(lo_ok, 1)

            for i in range(2):
                low(0, i)
            with pool.Fori(1, GROUPS // 2) as pair_of_groups:
                g = pair_of_groups * 2
                for i in range(2):
                    pool.wait_ge(kept[i], g * 16)
                    if router_w is not None:
                        pool.wait_ge(logit_ok, g + (i - 1))
                    low(g, i)
            if expert_w is not None:
                split_experts(range(E // PIECE))
                pool.wait_ge(w_lo_ok, E // PIECE)

        @block.vector
        def _(dve):
            done = [0]

            def chained(ins):
                done[0] += 1
                ins.then_inc(chain, 1)
                dve.wait_ge(chain, done[0])

            with dve.Fori(0, CHUNKS // UNROLL) as t:
                for c in range(UNROLL):
                    at = bass.ds(t * UNROLL + c, 1)
                    dve.bn_stats(stats[:, at, :].rearrange("p a s -> p (a s)"),
                                 k.x[:, at, :].rearrange("p a d -> p (a d)")).then_inc(stats_ok, 1)
            dve.wait_ge(stats_ok, CHUNKS)
            chained(dve.tensor_tensor(mean[:, :], stats[:, :, 1], stats[:, :, 4], ALU.add))
            chained(dve.tensor_tensor(diff[:, :], stats[:, :, 1], stats[:, :, 4], ALU.subtract))
            chained(dve.tensor_tensor(diff[:, :], diff[:, :], diff[:, :], ALU.mult))
            chained(dve.tensor_tensor(var[:, :], stats[:, :, 2], stats[:, :, 5], ALU.add))
            chained(dve.scalar_tensor_tensor(out=var[:, :], in0=diff[:, :], scalar=D / 4, in1=var[:, :],
                                             op0=ALU.mult, op1=ALU.add))
            dve.wait_ge(std_ok, 1)
            chained(dve.reciprocal(rstd[:, :], std[:, :]))
            chained(dve.scalar_tensor_tensor(out=shift[:, :], in0=mean[:, :], scalar=-0.5, in1=rstd[:, :],
                                             op0=ALU.mult, op1=ALU.mult))
            if router_w is not None:
                dve.wait_ge(rw_hi_ok, 1)
                dve.tensor_tensor(rT[:, 1, :], rT_ps[:, 0:E], f(rT[:, 0, :]), ALU.subtract).then_inc(rw_ok, 1)

            def normal(g, i):
                for c in range(GROUP):
                    at = bass.ds(g * GROUP + (i * GROUP + c), 1)
                    ins = dve.tensor_scalar(xn[i][:, c, :], k.x[:, at, :].rearrange("p a d -> p (a d)"),
                                            rstd[:, at], shift[:, at], ALU.mult, ALU.add)
                ins.then_inc(norm_ok, 1)

            for i in range(2):
                normal(0, i)
            with dve.Fori(1, GROUPS // 2) as pair_of_groups:
                g = pair_of_groups * 2
                for i in range(2):
                    dve.wait_ge(turn_ok, g + (i - 1))
                    normal(g, i)

            if router_w is not None:
                for i in range(2):
                    dve.wait_ge(logit_ok, (i + 1) * (GROUPS // 2))
                    lg = logit[:, i * HALF * 2 * E:(i + 1) * HALF * 2 * E].rearrange("p (c two e) -> p c two e", two=2, e=E)
                    weights = soft[i][:, :, 0:E]
                    row = lambda a: a[:, i, :].unsqueeze(2).to_broadcast([P, HALF, E])
                    chained(dve.tensor_copy(weights, lg[:, :, 0, :]))
                    chained(dve.tensor_tensor(weights, weights, lg[:, :, 1, :], ALU.add))
                    chained(dve.tensor_reduce(top[:, i, :], weights, AX.X, ALU.max))
                    dve.tensor_tensor(weights, weights, row(top), ALU.subtract).then_inc(shifted, 1)
                dve.wait_ge(none_ok, 2)
                for i in range(2):
                    row = lambda a: a[:, i, :].unsqueeze(2).to_broadcast([P, HALF, E])
                    weights = soft[i][:, :, 0:E]
                    dve.wait_ge(exp_ok, i + 1)
                    chained(dve.tensor_reduce(total[:, i, :], weights, AX.X, ALU.add))
                    chained(dve.reciprocal(total[:, i, :], total[:, i, :]))
                    chained(dve.tensor_tensor(weights, weights, row(total), ALU.mult))
                    for c in range(HALF):
                        ins = dve.max(best[i][:, c, :], weights[:, c, :])
                    chained(ins)
                    chained(dve.memset(best[i][:, :, 2:TOP], NONE))
                    for c in range(HALF):
                        ins = dve.match_replace(rest[i][:, c, :], best[i][:, c, :], soft[i][:, c, :], 0.0)
                    chained(ins)
                    chained(dve.tensor_tensor(k.gate[:, i * HALF:(i + 1) * HALF, :], weights, rest[i][:, :, 0:E], ALU.subtract))

        @block.scalar
        def _(act):
            if expert_w is not None:
                def round_experts(pieces):
                    for q in pieces:
                        act.wait_ge(w_in[q], 16)
                        at = slice(q * PIECE, (q + 1) * PIECE)
                        act.activation(k.w_hi[:, at, :], w_raw[:, at, :], ACT.Copy).then_inc(w_hi_ok, 1)
            if router_w is not None:
                act.wait_ge(rw_turned, 1)
                act.activation(rT[:, 0, :], rT_ps[:, 0:E], ACT.Copy).then_inc(rw_hi_ok, 1)
            act.wait_ge(chain, 5)
            act.activation(std[:, :], var[:, :], ACT.Sqrt, bias=k.eps[:, :], scale=1.0 / D).then_inc(std_ok, 1)
            def split(g, i):
                act.wait_ge(turn_ok, g + (i + 1))
                act.activation(hi[i][:, :], turned[i][:, :], ACT.Copy).then_inc(hi_ok, 1)
                act.activation(raw[i][:, :], turned[i][:, :], ACT.Copy).then_inc(raw_ok, 1)

            for i in range(2):
                split(0, i)
            with act.Fori(1, GROUPS // 2) as pair_of_groups:
                g = pair_of_groups * 2
                for i in range(2):
                    act.wait_ge(kept[i], g * 16)
                    act.wait_ge(lo_ok, g + (i - 1))
                    if router_w is not None:
                        act.wait_ge(logit_ok, g + (i - 1))
                    split(g, i)
            if router_w is not None:
                for i in range(2):
                    act.wait_ge(shifted, i + 1)
                    act.activation(soft[i][:, :, 0:E], soft[i][:, :, 0:E], ACT.Exp).then_inc(exp_ok, 1)
            if expert_w is not None:
                round_experts(range(E // PIECE))

        @block.tensor
        def _(pe):
            if router_w is not None:
                pe.wait_ge(rw_in, 16)
                pe.transpose(rT_ps[:, 0:E], rw_raw[:, :], k.ident[0:E, 0:E]).then_inc(rw_turned, 1)

            def turn(g, i):
                pe.wait_ge(norm_ok, g + (i + 1))
                for c in range(GROUP):
                    ins = pe.transpose(turned[i][:, c * P:(c + 1) * P], xn[i][:, c, :], k.ident[:, :])
                ins.then_inc(turn_ok, 1)

            def route(g, i):
                pe.wait_ge(lo_ok, g + (i + 1))
                for c in range(GROUP):
                    at = slice(c * P, (c + 1) * P)
                    out = g * (GROUP * 2 * E) + (i * GROUP + c) * 2 * E
                    pe.matmul(logit[:, bass.ds(out, 2 * E)], hi[i][:, at], rT[:, :, :].rearrange("p a e -> p (a e)"),
                              start=True, stop=False, skip_group_check=True)
                    ins = pe.matmul(logit[:, bass.ds(out, E)], lo[i][:, at], rT[:, 0, :],
                                    start=False, stop=True, skip_group_check=True)
                ins.then_inc(logit_ok, 1)

            for i in range(2):
                turn(0, i)
            if router_w is not None:
                pe.wait_ge(rw_ok, 1)
            with pe.Fori(1, GROUPS // 2) as pair_of_groups:
                g = pair_of_groups * 2
                for i in range(2):
                    pe.wait_ge(raw_ok, g + (i - 1))
                    turn(g, i)
                    if router_w is not None:
                        route(g - 2, i)
            if router_w is not None:
                for i in range(2):
                    route(GROUPS - 2, i)


class Rounds:

    def __init__(self, engine, sem, per, scratch):
        self.engine, self.sem, self.per, self.scratch = engine, sem, per, scratch
        self.fixed = -per
        self.base = engine.alloc_register(f"round_of_{sem.name}")
        engine.reg_mov(self.base, 0)

    def _wait(self, n):
        if self.fixed is not None:
            self.engine.wait_ge(self.sem, self.fixed + n)
        else:
            self.engine.reg_add(self.scratch, self.base, n)
            self.engine.wait_ge(self.sem, self.scratch)

    def now(self, n):
        self._wait(self.per + n + 1)

    def before(self, n):
        self._wait(n + 1)

    def at(self, n):
        self._wait(self.per + n + 1)

    def enter_loop(self):
        self.fixed = None

    def forward(self):
        self.engine.reg_add(self.base, self.base, self.per)

    def leave_loop(self, rounds, not_done=0):
        self.fixed = rounds * self.per - not_done


def experts(nc, k, phase):
    E = 32
    PER = 4
    BANKS = 8
    QUADS = E // PER
    ROUNDS = GROUPS // 2
    PAIRS = GROUP // 2
    FILLS = 2 * QUADS
    DVE_SUMS = QUADS * PER
    WEIGHED = QUADS
    POOL_SUMS = 10
    FOLD = 6
    READ_AT = [0, 1, 0, 1, 2, 3, 4, 5]
    with ExitStack() as stack:
        s = Scope(nc, stack, phase)
        xs_hi = [s.sb(f"xs_hi{i}", [P, GT], F32R) for i in range(2)]
        xs_lo = [s.sb(f"xs_lo{i}", [P, GT], F32R) for i in range(2)]
        acc = [s.sb(f"acc{i}", [P, GROUP, D]) for i in range(2)]
        gate = [s.sb(f"gate{i}", [P, GROUP, E]) for i in range(2)]
        weighed = [s.sb(f"weighed{n}", [P, PER, D]) for n in range(WEIGHED)]
        quad_sum = [s.sb(f"quad_sum{n}", [P, PER, D]) for n in range(2)]
        folded = [s.sb(f"folded{n}", [P, 2, D]) for n in range(2)]
        odd_sum = [s.sb(f"odd_sum{i}", [P, GROUP, D]) for i in range(2)]
        y = [s.ps(f"y{i}") for i in range(BANKS)]
        mm_ok, dve_sum, weighed_ok, pool_sum, gate_in, merged = (s.sem(n) for n in (
            "mm_ok", "dve_sum", "weighed_ok", "pool_sum", "gate_in", "merged"))
        xs_in = [s.sem(f"xs_in{i}") for i in range(2)]
        PAIR = {id(mm_ok): FILLS, id(dve_sum): DVE_SUMS, id(weighed_ok): WEIGHED, id(pool_sum): POOL_SUMS}
        PER_ROUND = {x: n * PAIRS * 2 for x, n in PAIR.items()}
        PER_ROUND.update({id(gate_in): 2, id(merged): 2})

        def rounds(engine, *sems):
            scratch = engine.alloc_register(f"{phase}_value_{engine.engine.name}")
            return [Rounds(engine, x, PER_ROUND[id(x)], scratch) for x in sems]

        def in_pair(r, i, pair, n):
            r.at((i * PAIRS + pair) * PAIR[id(r.sem)] + n)

        block = s.block()

        @block.sync
        def _(sync):
            def fetch(g, i):
                sync.dma_start(f(xs_hi[i][:, :]), k.xT_hi[:, bass.ds(g * GT + i * GT, GT)]).then_inc(xs_in[i], 16)
                sync.dma_start(f(xs_lo[i][:, :]), k.xT_lo[:, bass.ds(g * GT + i * GT, GT)]).then_inc(xs_in[i], 16)
            MM, = rounds(sync, mm_ok)
            MM.enter_loop()
            for i in range(2):
                fetch(0, i)
            with sync.Fori(1, ROUNDS) as r:
                for i in range(2):
                    in_pair(MM, i, PAIRS - 1, FILLS - 1)
                    fetch(r * 2, i)
                MM.forward()

        @block.gpsimd
        def _(pool):
            for x in (pool_sum, gate_in):
                pool.sem_inc(x, PER_ROUND[id(x)])
            W, M, S, DS = waits = rounds(pool, weighed_ok, merged, pool_sum, dve_sum)
            for x in waits:
                x.enter_loop()

            def gates(r, i):
                pool.tensor_copy(gate[i][:, :, :], k.gate[:, bass.ds(r * (2 * GROUP) + i * GROUP, GROUP), :]).then_inc(gate_in, 1)

            gates(0, 0)
            with pool.Fori(0, ROUNDS) as r:
                for i in range(2):
                    for pair in range(PAIRS):
                        if pair == PAIRS - 1:
                            in_pair(W, i - 1, PAIRS - 1, WEIGHED - 1)
                            in_pair(DS, i - 1, PAIRS - 1, DVE_SUMS - 1)
                            gates((r + i) & (ROUNDS - 1), 1 - i)
                        for quad in range(1, QUADS // 2):
                            for odd in range(2):
                                total = quad_sum[odd][:, :, :].rearrange("p e d -> p (e d)")
                                n = 2 * quad + odd
                                in_pair(W, i, pair, n)
                                in_pair(S, i, pair, 2 * (quad - 1) - 2 + odd if quad > 1 else FOLD + odd - POOL_SUMS)
                                have = weighed[odd][:, :, :].rearrange("p e d -> p (e d)") if quad == 1 else total
                                pool.tensor_tensor(total, have, weighed[n][:, :, :].rearrange("p e d -> p (e d)"),
                                                   ALU.add).then_inc(pool_sum, 1)
                        for odd in range(2):
                            in_pair(S, i, pair, FOLD - 2 + odd)
                            in_pair(S, i, pair, FOLD + 2 + odd - POOL_SUMS)
                            pool.tensor_tensor(folded[odd][:, :, :], quad_sum[odd][:, 0:2, :], quad_sum[odd][:, 2:4, :],
                                               ALU.add).then_inc(pool_sum, 1)
                        for odd in range(2):
                            in_pair(S, i, pair, FOLD + odd)
                            M.at(i - 2)
                            pool.tensor_tensor(odd_sum[i][:, 2 * pair + odd, :], folded[odd][:, 0, :],
                                               folded[odd][:, 1, :], ALU.add).then_inc(pool_sum, 1)
                for x in waits:
                    x.forward()

        @block.scalar
        def _(act):
            act.sem_inc(weighed_ok, PER_ROUND[id(weighed_ok)])
            MM, PS, GA = waits = rounds(act, mm_ok, pool_sum, gate_in)
            for x in waits:
                x.enter_loop()
            with act.Fori(0, ROUNDS) as _:
                for i in range(2):
                    GA.at(i)
                    for pair in range(PAIRS):
                        for quad in range(1, QUADS, 2):
                            for odd in range(2):
                                n = quad // 2 * 2 + odd
                                in_pair(MM, i, pair, 2 * quad + odd)
                                in_pair(PS, i, pair, READ_AT[n] - POOL_SUMS)
                                for e in range(PER):
                                    g = gate[i][:, 2 * pair + odd, quad * PER + e:quad * PER + e + 1]
                                    ins = act.activation(weighed[n][:, e, :], y[(2 * quad + odd) % BANKS][:, e * D:(e + 1) * D],
                                                         ACT.Copy, scale=g)
                                ins.then_inc(weighed_ok, 1)
                for x in waits:
                    x.forward()

        @block.vector
        def _(dve):
            dve.sem_inc(dve_sum, PER_ROUND[id(dve_sum)])
            dve.sem_inc(merged, PER_ROUND[id(merged)])
            MM, DS, GA, PS, M = waits = rounds(dve, mm_ok, dve_sum, gate_in, pool_sum, merged)

            def sums(g, r, pair):
                i = g % 2
                for quad in range(0, QUADS, 2):
                    for e in range(PER):
                        for odd in range(2):
                            if e == 0:
                                in_pair(MM, g, pair, 2 * quad + odd)
                            n = quad // 2 * 2 * PER + 2 * e + odd
                            c = 2 * pair + odd
                            if n >= 2:
                                in_pair(DS, g, pair, n - 2)
                                have = acc[i][:, c, :]
                            else:
                                M.at(g - 2)
                                have = k.x[:, bass.ds(r * (2 * GROUP) + (g * GROUP + c), 1), :].rearrange("p a d -> p (a d)")
                            dve.scalar_tensor_tensor(
                                out=acc[i][:, c, :], in0=y[(2 * quad + odd) % BANKS][:, e * D:(e + 1) * D],
                                scalar=gate[i][:, c, quad * PER + e:quad * PER + e + 1], in1=have,
                                op0=ALU.mult, op1=ALU.add).then_inc(dve_sum, 1)

            def merge(g, r):
                in_pair(PS, g, PAIRS - 1, POOL_SUMS - 1)
                in_pair(DS, g, PAIRS - 1, DVE_SUMS - 1)
                dve.tensor_tensor(k.x[:, bass.ds(r * (2 * GROUP) + g * GROUP, GROUP), :], acc[g % 2][:, :, :],
                                  odd_sum[g % 2][:, :, :], ALU.add).then_inc(merged, 1)

            def group(g, r, last=False):
                for pair in range(PAIRS):
                    if pair == 0:
                        GA.at(g)
                    if pair == 1 and not (g == 0 and isinstance(r, int) and r == 0):
                        merge(g - 1, r)
                    sums(g, r, pair)

            for x in waits:
                x.fixed = 0
            group(0, 0)
            for x in waits:
                x.enter_loop()
            with dve.Fori(0, ROUNDS - 1) as r:
                for g in (1, 2):
                    group(g, r)
                for x in waits:
                    x.forward()
            for x in waits:
                x.fixed = (ROUNDS - 1) * x.per
            group(1, ROUNDS - 1)
            merge(1, ROUNDS - 1)

        @block.tensor
        def _(pe):
            pe.sem_inc(mm_ok, PER_ROUND[id(mm_ok)])
            DS, W = waits = rounds(pe, dve_sum, weighed_ok)
            xs_count = pe.alloc_register(f"{phase}_xs_count")
            pe.reg_mov(xs_count, 0)
            for x in waits:
                x.enter_loop()
            with pe.Fori(0, ROUNDS) as _:
                pe.reg_add(xs_count, xs_count, 32)
                for i in range(2):
                    pe.wait_ge(xs_in[i], xs_count)
                    for pair in range(PAIRS):
                        for quad in range(QUADS):
                            for odd in range(2):
                                if quad % 2:
                                    in_pair(W, i, pair, (quad - 4) // 2 * 2 + odd)
                                else:
                                    in_pair(DS, i, pair, (quad - 4) // 2 * 2 * PER + 2 * (PER - 1) + odd)
                                at = slice((2 * pair + odd) * P, (2 * pair + odd + 1) * P)
                                out = y[(2 * quad + odd) % BANKS][:, :]
                                hi = k.w_hi[:, quad * PER:(quad + 1) * PER, :].rearrange("h e d -> h (e d)")
                                lo = k.w_lo[:, quad * PER:(quad + 1) * PER, :].rearrange("h e d -> h (e d)")
                                pe.matmul(out, xs_hi[i][:, at], hi, start=True, stop=False)
                                pe.matmul(out, xs_hi[i][:, at], lo, start=False, stop=False)
                                pe.matmul(out, xs_lo[i][:, at], hi, start=False, stop=True).then_inc(mm_ok, 1)
                for x in waits:
                    x.forward()


def attention(nc, k, wq_dram, wkv_dram, wo_dram, bo_dram):
    H, DH = 16, 64
    PAIRS = H // 2
    ROUNDS = B * PAIRS
    BLOCKS = N // P
    SLOTS = 2 * BLOCKS
    HALF = 512
    SCALE = DH ** -0.5
    SUM_EPS = 1e-8
    MASKED = -1e30
    RING = 4
    TURN = SLOTS
    TURN_SLOT = 6
    V_UNITS, SCALE_UNITS, OUT_UNITS = (0, 6), (7, 8), (9, 11)
    QK_B, QK_A = (3, 4), (12, 13)
    QK_UNITS = QK_B + QK_A
    UNIT_ORDER = sorted([*V_UNITS, *QK_UNITS, TURN, *SCALE_UNITS, *OUT_UNITS],
                        key=lambda u: TURN_SLOT + 0.5 if u == TURN else u)
    UNITS = len(UNIT_ORDER)
    Q, K = 0, 1
    SCALE_LO = 32
    PLACE = {slot: n for n, slot in enumerate(UNIT_ORDER)}
    SPLIT = {QK_B[0]: 1, QK_B[1]: 3, TURN: 4, QK_A[0]: 6, QK_A[1]: 8}
    SPLITS = 9
    NOT_DONE = PLACE[TURN]
    IN_TURN = (QK_B[0], QK_A[0])
    UNIT_LATE = QK_UNITS
    PV_AT = {2: (0, 1, range(0, 2)), 3: (0, 1, range(2, 4)), 4: (0, 1, range(4, 6)), 5: (0, 1, range(6, 8)),
             14: (1, 0, range(0, 1)), 15: (1, 0, range(1, 4))}
    PV_DONE = {5: (0, 1), 15: (1, 0)}

    def unit_before(u):
        same = [x for x in UNIT_ORDER if x != TURN and (x in IN_TURN) == (u in IN_TURN)]
        n = same.index(u)
        return same[n - 1], n == 0

    def projection(u):
        return int(u in QK_B), QK_UNITS.index(u) % 2

    def turned_slot(s):
        t = (s - 2) % SLOTS
        return t // BLOCKS, t % BLOCKS

    with ExitStack() as stack:
        s_ = Scope(nc, stack, "attn")
        sb, ps, sem = s_.sb, s_.ps, s_.sem
        xs_hi, xs_lo = sb("xs_hi", [P, N], F32R), sb("xs_lo", [P, N], F32R)
        w_raw = sb("w_raw", [P, 2, H * DH])
        wv_hi, wv_lo = sb("wv_hi", [P, H * DH], F32R), sb("wv_lo", [P, H * DH], F32R)
        w_hi = [sb(f"w_hi{h}", [P, 2, DH], F32R) for h in range(2)]
        w_lo = [sb(f"w_lo{h}", [P, 2, DH], F32R) for h in range(2)]
        wo, wo_now = sb("wo", [P, PAIRS, D]), sb("wo_now", [P, D])
        yT = sb("yT", [P, T])
        bo = sb("bo", [P, 1])
        q_both = [sb(f"q_both{h}", [P, N], F32R) for h in range(2)]
        k_hi = [sb(f"k_hi{h}", [P, N], F32R) for h in range(2)]
        k_lo = [sb(f"k_lo{h}", [P, N], F32R) for h in range(2)]
        v = sb("v", [P, BLOCKS, 2, DH])
        v_next = sb("v_next", [P, BLOCKS, 2, DH])
        prob = [sb(f"prob{i}", [P, N]) for i in range(RING)]
        prob_t = [[sb(f"prob_t{h}{u}", [P, 4 * (u + 1), HALF]) for u in range(2)] for h in range(2)]
        o = sb("o", [P, N])
        o_norm = sb("o_norm", [P, N])
        neg_max = sb("neg_max", [P, RING])
        one = sb("one", [P, 1])
        row_sum, row_inv = sb("row_sum", [P, SLOTS]), sb("row_inv", [P, SLOTS])
        scale = sb("scale", [SCALE_LO + SLOTS, P], F32R)
        pick = sb("pick", [SCALE_LO + SLOTS, BLOCKS, P], F32R)
        causal = sb("causal", [P, P])

        score = [ps(f"score{i}", (P, N)) for i in range(2)]
        turn = ps("turn", (P, N))
        pv = ps("pv")
        unit_bank = ps("unit")

        def bank(u):
            if u == TURN:
                return pv[:, :]
            return turn[:, HALF:N] if u in IN_TURN else unit_bank[:, :]

        s_ok, masked, exp_ok, turned, turn_out, pv_ok, o_ok, inv_ok, unit_ok, half_ok, unit_free, w_ok, v_ok, wo_ok, twice_ok = (
            sem(n) for n in ("s_ok", "masked", "exp_ok", "turned", "turn_out", "pv_ok", "o_ok", "inv_ok",
                             "unit_ok", "half_ok", "unit_free", "w_ok", "v_ok", "wo_ok", "twice_ok"))
        back_ok, x_ok = sem("back_ok"), sem("x_ok")
        PER = {id(s_ok): 16, id(masked): 16, id(exp_ok): 16, id(turned): 16, id(turn_out): 16, id(v_ok): 1, id(wo_ok): 1,
               id(pv_ok): 2, id(o_ok): 2, id(inv_ok): 2, id(unit_ok): UNITS, id(half_ok): SPLITS,
               id(twice_ok): 2 * len(QK_UNITS),
               id(unit_free): UNITS, id(w_ok): 2}
        wqk_in, wv_in, wo_in, bo_in, xs_in = (sem(n) for n in ("wqk_in", "wv_in", "wo_in", "bo_in", "xs_in"))
        scaled, wv_hi_ok, wv_ok, consts, primed, w_half, zeroed, maxed, summed, biased = (sem(n) for n in (
            "scaled", "wv_hi_ok", "wv_ok", "consts", "primed", "w_half", "zeroed", "maxed", "summed", "biased"))
        block = s_.block()
        pick_raw = o_norm[0:SCALE_LO + SLOTS, :].rearrange("p (b m) -> p b m", m=P)
        wv_raw = prob_t[1][0][:, 0:2, :].rearrange("p a b -> p (a b)")

        def rounds(engine, *sems):
            scratch = engine.alloc_register(f"wait_value_{engine.engine.name}")
            return [Rounds(engine, x, PER[id(x)], scratch) for x in sems]

        @block.sync
        def _(sync):
            sync.dma_start(w_raw[:, 0, :], wq_dram).then_inc(wqk_in, 16)
            sync.dma_start(w_raw[:, 1, :], wkv_dram[:, 0:H * DH]).then_inc(wqk_in, 16)
            sync.dma_start(wv_raw, wkv_dram[:, H * DH:2 * H * DH]).then_inc(wv_in, 16)
            sync.dma_start(f(xs_hi[:, :]), k.xT_hi[:, 0:N]).then_inc(xs_in, 16)
            sync.dma_start(f(xs_lo[:, :]), k.xT_lo[:, 0:N]).then_inc(xs_in, 16)
            sync.dma_start(bo[:, :], bo_dram.rearrange("(n a) -> n a", a=1)).then_inc(bo_in, 16)
            sync.dma_start(wo[:, :, :], wo_dram.rearrange("(h p) n -> p h n", p=P)).then_inc(wo_in, 16)
            units, = rounds(sync, unit_ok)
            units.enter_loop()
            with sync.Fori(0, ROUNDS) as it:
                units.now(PLACE[V_UNITS[1]])
                at = (((it + 1) >> 3) & (B - 1)) * N
                sync.dma_start(f(xs_hi[:, :]), k.xT_hi[:, bass.ds(at, N)]).then_inc(xs_in, 16)
                sync.dma_start(f(xs_lo[:, :]), k.xT_lo[:, bass.ds(at, N)]).then_inc(xs_in, 16)
                units.forward()

        @block.gpsimd
        def _(pool):
            pool.sem_inc(v_ok, 1)
            halves = pool.alloc_register("w_half_count")
            pool.reg_mov(halves, 1)
            pool.sem_inc(twice_ok, 4)
            U, F, V, W, WO, TW = rounds(pool, unit_ok, unit_free, pv_ok, w_ok, wo_ok, twice_ok)

            def prepare(h, pair):
                src = w_raw[:, :, bass.ds(pair * (2 * DH) + h * DH, DH)]
                pool.tensor_copy(w_hi[h][:, :, :], src).then_inc(w_half, 1)
                pool.wait_ge(w_half, halves)
                pool.reg_add(halves, halves, 1)
                pool.tensor_tensor(w_lo[h][:, :, :], src, f(w_hi[h][:, :, :]), ALU.subtract).then_inc(w_ok, 1)

            def twice(u):
                h, half = projection(u)
                at = slice(half * HALF, (half + 1) * HALF)
                F.now(PLACE[u])
                for n, part in enumerate((k_hi[h], k_lo[h])):
                    pool.tensor_tensor(part[0:DH, at], f(part[DH:P, at]), one[DH:P, :].to_broadcast([DH, HALF]),
                                       ALU.mult).then_inc(twice_ok, 1)
                    TW.now(2 * QK_UNITS.index(u) + n)

            pool.memset(causal[:, :], 0.0).then_inc(zeroed, 1)
            pool.memset(pick_raw[:, :, :], 0.0).then_inc(zeroed, 1)
            pool.wait_ge(zeroed, 2)
            pool.affine_select(out=causal[:, :], in_=causal[:, :], compare_op=ALU.is_ge, fill=MASKED, base=0,
                               pattern=[[-1, P]], channel_multiplier=1).then_inc(consts, 1)
            by_head = pick_raw[:, :, :].rearrange("k b (h m) -> k b h m", h=2)
            for n in range(2):
                pool.affine_select(out=by_head, in_=by_head, compare_op=ALU.not_equal, fill=1.0, base=-n * SCALE_LO,
                                   pattern=[[-1, BLOCKS], [-BLOCKS, 2], [0, DH]], channel_multiplier=1
                                   ).then_inc(consts if n else zeroed, 1)
                if n == 0:
                    pool.wait_ge(zeroed, 3)
            pool.memset(f(scale[:, :]), 0.0).then_inc(primed, 1)
            for t in (prob[2], o, neg_max):
                pool.memset(t[:, :], 0.0).then_inc(primed, 1)
            pool.memset(row_sum[:, :], 1.0).then_inc(primed, 1)
            pool.memset(row_inv[:, :], 1.0).then_inc(primed, 1)
            pool.memset(one[:, :], 1.0).then_inc(primed, 1)
            pool.wait_ge(scaled, 1)
            pool.wait_ge(wqk_in, 32)
            prepare(0, 0)
            prepare(1, 0)
            pool.memset(prob_t[1][1][:, :, :], 0.0).then_inc(primed, 1)
            pool.memset(v[:, :, :, :], 0.0).then_inc(primed, 1)
            pool.wait_ge(consts, 3)
            pool.memset(o_norm[:, :], 0.0).then_inc(primed, 1)
            pool.wait_ge(primed, 12)
            twice(QK_A[0])
            twice(QK_A[1])
            for r in (U, F, V, W, WO, TW):
                r.enter_loop()
            pool.sem_inc(wo_ok, 1)
            pool.wait_ge(wo_in, 16)
            with pool.Fori(0, ROUNDS) as it:
                pair = (it + 1) & (PAIRS - 1)
                U.before(PLACE[QK_A[1]])
                prepare(0, pair)
                U.before(PLACE[OUT_UNITS[1]])
                pool.tensor_copy(wo_now[:, :], wo[:, bass.ds((it + (PAIRS - 1)) & (PAIRS - 1), 1), :]
                                 .rearrange("p a d -> p (a d)")).then_inc(wo_ok, 1)
                WO.now(0)
                twice(QK_B[0])
                twice(QK_B[1])
                F.now(PLACE[V_UNITS[1]])
                V.now(0)
                flat = v_next[:, :, :, :].rearrange("p j h d -> p (j h d)")
                pool.tensor_tensor(v[:, :, :, :].rearrange("p j h d -> p (j h d)"), flat,
                                   one[:, :].to_broadcast([P, BLOCKS * 2 * DH]), ALU.mult).then_inc(v_ok, 1)
                prepare(1, pair)
                W.now(1)
                twice(QK_A[0])
                twice(QK_A[1])
                for r in (U, F, V, W, WO, TW):
                    r.forward()
            U.leave_loop(ROUNDS)
            U.before(PLACE[OUT_UNITS[1]])
            pool.tensor_copy(wo_now[:, :], wo[:, PAIRS - 1, :]).then_inc(wo_ok, 1)

        @block.scalar
        def _(act):
            act.sem_inc(exp_ok, 16)
            act.sem_inc(turn_out, 16)
            act.sem_inc(o_ok, 2)
            act.sem_inc(half_ok, SPLIT[TURN] + 1)
            S, M, T, V, I, U, F = rounds(act, s_ok, masked, turned, pv_ok, inv_ok, unit_ok, unit_free)
            act.wait_ge(wqk_in, 32)
            act.activation(w_raw[:, Q, :], w_raw[:, Q, :], ACT.Copy, scale=SCALE).then_inc(scaled, 1)
            act.wait_ge(wv_in, 16)
            act.activation(wv_hi[:, :], wv_raw, ACT.Copy).then_inc(wv_hi_ok, 1)
            act.wait_ge(consts, 2)
            act.activation(pick[:, :, :], pick_raw[:, :, :], ACT.Copy).then_inc(consts, 1)
            act.wait_ge(bo_in, 16)
            act.activation(yT[:, :], bo[:, :].to_broadcast([P, B * N]), ACT.Copy).then_inc(biased, 1)

            def copy_turned(s):
                h, b = turned_slot(s)
                T.now(s)
                if s == 2:
                    V.before(1)
                if s == 6:
                    V.now(0)
                n = b + 1
                act.activation(prob_t[h][b // 4][:, 0:n, (b % 4) * P:(b % 4 + 1) * P],
                               turn[:, 0:n * P].rearrange("p (j i) -> p j i", j=n), ACT.Copy).then_inc(turn_out, 1)

            def exponentials(slot):
                s = (slot - 1) % SLOTS
                b = s % BLOCKS
                M.now(s) if slot else M.before(s)
                T.now(slot - 3) if slot >= 3 else T.before(slot + 13)
                if s in (0, 8):
                    I.before(1) if s == 0 else I.now(0)
                w = (b + 1) * P
                act.activation(prob[s % RING][:, 0:w], score[s % 2][:, 0:w], ACT.Exp,
                               bias=neg_max[:, s % RING:s % RING + 1],
                               accum_out=row_sum[:, s:s + 1]).then_inc(exp_ok, 1)

            def unit_out(u, first=False):
                if u not in SPLIT:
                    return
                U.now(PLACE[u])
                if u == TURN:
                    act.activation(scale[0:SLOTS, :], bank(u)[0:SLOTS, 0:P], ACT.Copy).then_inc(half_ok, 1)
                else:
                    h, half = projection(u)
                    if not first:
                        S.before(15) if h else S.now(7)
                    at = slice(half * HALF, (half + 1) * HALF)
                    act.activation(q_both[h][0:DH, at], bank(u)[0:DH, :], ACT.Copy).then_inc(half_ok, 1)
                    act.activation(k_hi[h][DH:P, at], bank(u)[DH:P, :], ACT.Copy).then_inc(half_ok, 1)

            def product_out(s):
                n, half = PV_DONE[s]
                V.now(n)
                F.now(PLACE[SCALE_UNITS[0]]) if half == 0 else F.before(PLACE[SCALE_UNITS[1]])
                act.activation(o[:, half * HALF:(half + 1) * HALF], pv[:, :], ACT.Copy).then_inc(o_ok, 1)

            def forward():
                for r in (S, M, T, V, I, U, F):
                    r.forward()

            for u in QK_A:
                unit_out(u, first=True)
            for r in (S, M, T, V, I, U, F):
                r.enter_loop()
            act.wait_ge(primed, 12)
            with act.Fori(0, ROUNDS) as _:
                for s in range(SLOTS):
                    if s in PLACE:
                        unit_out(s)
                    exponentials(s)
                    if s == TURN_SLOT:
                        unit_out(TURN)
                    copy_turned(s)
                    if s in PV_DONE:
                        product_out(s)
                forward()
            for r in (M, T, V, F):
                r.leave_loop(ROUNDS)
            U.leave_loop(ROUNDS, NOT_DONE)
            exponentials(0)
            copy_turned(0)
            copy_turned(1)
            product_out(5)
            unit_out(TURN)

        @block.vector
        def _(dve):
            dve.sem_inc(masked, 16)
            dve.sem_inc(inv_ok, 2)
            dve.sem_inc(unit_free, PLACE[QK_A[0]])
            S, E, O, U, HF, F, VC = rounds(dve, s_ok, exp_ok, o_ok, unit_ok, half_ok, unit_free, v_ok)
            dve.memset(score[1][:, :], 0.0).then_inc(primed, 1)
            dve.memset(prob_t[0][1][:, :, :], 0.0).then_inc(primed, 1)
            dve.wait_ge(wv_hi_ok, 1)
            dve.tensor_tensor(wv_lo[:, :], wv_raw, f(wv_hi[:, :]), ALU.subtract).then_inc(wv_ok, 1)
            max_count, sum_count = dve.alloc_register("max_count"), dve.alloc_register("sum_count")
            dve.reg_mov(max_count, 0)
            dve.reg_mov(sum_count, 0)

            def maxima(s):
                b = s % BLOCKS
                S.now(s)
                dve.tensor_reduce(neg_max[:, s % RING:s % RING + 1], score[s % 2][:, :], AX.X, ALU.max,
                                  negate=True).then_inc(maxed, 1)
                dve.reg_add(max_count, max_count, 1)
                dve.wait_ge(maxed, max_count)
                diag = score[s % 2][:, b * P:(b + 1) * P]
                dve.tensor_tensor(diag, diag, causal[:, :], ALU.add).then_inc(masked, 1)

            def inverses(h):
                E.now(0) if h else E.now(8)
                if not h:
                    U.now(PLACE[TURN])
                cols = slice(h * BLOCKS, (h + 1) * BLOCKS)
                dve.tensor_scalar(row_sum[:, cols], row_sum[:, cols], SUM_EPS, None, ALU.add).then_inc(summed, 1)
                dve.reg_add(sum_count, sum_count, 1)
                dve.wait_ge(summed, sum_count)
                dve.reciprocal(row_inv[:, cols], row_sum[:, cols]).then_inc(inv_ok, 1)

            def unit_out(u, round_before=None):
                if u in SPLIT:
                    HF.now(SPLIT[u])
                else:
                    U.now(PLACE[u])
                if u in V_UNITS:
                    if u == V_UNITS[0]:
                        VC.before(0)
                    n = V_UNITS.index(u)
                    at = slice(n * 4, (n + 1) * 4)
                    dve.tensor_copy(v_next[:, at, :, :].rearrange("p j h d -> p (j h d)"), bank(u)).then_inc(unit_free, 1)
                elif u == TURN:
                    dve.tensor_tensor(scale[SCALE_LO:SCALE_LO + SLOTS, :], bank(u)[0:SLOTS, 0:P], f(scale[0:SLOTS, :]),
                                      ALU.subtract).then_inc(unit_free, 1)
                elif u in SCALE_UNITS:
                    n = SCALE_UNITS.index(u)
                    O.now(0) if n else O.before(1)
                    at = slice(n * HALF, (n + 1) * HALF)
                    dve.tensor_tensor(o_norm[:, at], bank(u), o[:, at], ALU.mult).then_inc(unit_free, 1)
                elif u in OUT_UNITS:
                    F.before(PLACE[u])
                    y = yT[:, bass.ds(((round_before >> 3) & (B - 1)) * N + OUT_UNITS.index(u) * HALF, HALF)]
                    dve.tensor_tensor(y, bank(u), y, ALU.add).then_inc(unit_free, 1)
                else:
                    h, half = projection(u)
                    at = slice(half * HALF, (half + 1) * HALF)
                    dve.tensor_tensor(q_both[h][DH:P, at], bank(u)[0:DH, :], f(q_both[h][0:DH, at]), ALU.subtract)
                    dve.tensor_tensor(k_lo[h][DH:P, at], bank(u)[DH:P, :], f(k_hi[h][DH:P, at]),
                                      ALU.subtract).then_inc(unit_free, 1)

            def forward():
                for r in (S, E, O, U, HF, F, VC):
                    r.forward()

            for u in QK_A:
                unit_out(u)
            for r in (S, E, O, U, HF, F, VC):
                r.enter_loop()
            dve.wait_ge(primed, 12)
            dve.wait_ge(consts, 3)
            dve.wait_ge(biased, 1)
            with dve.Fori(0, ROUNDS) as it:
                for s in range(SLOTS):
                    if s in UNIT_LATE:
                        maxima(s)
                    if s in PLACE:
                        unit_out(s, (it + (ROUNDS - 1)) & (ROUNDS - 1))
                    if s not in UNIT_LATE:
                        maxima(s)
                    if s == TURN_SLOT:
                        unit_out(TURN)
                    if s in (1, 9):
                        inverses(int(s == 1))
                forward()
            for r in (E, O, F):
                r.leave_loop(ROUNDS)
            U.leave_loop(ROUNDS, NOT_DONE)
            HF.leave_loop(ROUNDS, SPLIT[QK_B[1]] + 1)
            inverses(1)
            for u in (TURN, *SCALE_UNITS, *OUT_UNITS):
                unit_out(u, ROUNDS - 1)
            for g in range(GROUPS):
                dve.wait_ge(back_ok, g + 1)
                x = k.x[:, g * GROUP:(g + 1) * GROUP, :].rearrange("p c d -> p (c d)")
                at = slice(g % 2 * HALF, (g % 2 + 1) * HALF)
                dve.tensor_tensor(x, score[g // 2 % 2][:, at], x, ALU.add).then_inc(x_ok, 1)

        @block.tensor
        def _(pe):
            pe.sem_inc(s_ok, 16)
            pe.sem_inc(turned, 16)
            pe.sem_inc(pv_ok, 2)
            pe.sem_inc(unit_ok, PLACE[QK_A[0]])
            E, TO, O, I, F, W, VC, WO, TW = rounds(pe, exp_ok, turn_out, o_ok, inv_ok, unit_free, w_ok, v_ok, wo_ok, twice_ok)
            xs_count = pe.alloc_register("xs_count")
            pe.reg_mov(xs_count, 32)

            def scores(s):
                h, b = s // BLOCKS, s % BLOCKS
                if b == 0:
                    TW.now(3) if h else TW.before(7)
                E.now(s - 1) if s else E.before(15)
                q = q_both[h][:, b * P:(b + 1) * P]
                for half in range(2):
                    at = slice(half * HALF, (half + 1) * HALF)
                    pe.matmul(score[s % 2][:, at], q, k_hi[h][:, at], start=True, stop=False)
                    ins = pe.matmul(score[s % 2][:, at], q, k_lo[h][:, at], start=False, stop=True)
                ins.then_inc(s_ok, 1)

            def turn_round(s):
                h, b = turned_slot(s)
                E.now(s - 1) if s else E.before(15)
                TO.now(s - 1) if s else TO.before(15)
                if s in (6, 14):
                    F.now(PLACE[IN_TURN[s // 8]])
                src = prob[(s - 2) % RING]
                for j in range(b + 1):
                    ins = pe.transpose(turn[:, j * P:(j + 1) * P], src[:, j * P:(j + 1) * P], k.ident[:, :])
                ins.then_inc(turned, 1)

            def product(s):
                n, half, blocks = PV_AT[s]
                if s == 2:
                    VC.before(0)
                    O.before(1)
                    TO.now(1)
                elif s == 14:
                    VC.now(0)
                    O.now(0)
                    F.now(PLACE[TURN])
                    TO.now(13)
                for j in blocks:
                    at = slice(max(0, j * P - half * HALF), HALF)
                    for h in range(2):
                        ins = pe.matmul(pv[h * DH:(h + 1) * DH, at], v[:, j, h, :], prob_t[h][half][:, j, at],
                                        start=(j == 0), stop=(j == 4 * half + 3))
                if s in PV_DONE:
                    ins.then_inc(pv_ok, 1)

            def one_unit(u, pair=None, first=False):
                if u == TURN:
                    O.now(0)
                else:
                    earlier, past = unit_before(u)
                    if not (first and u in (SCALE_UNITS[0], *QK_A)):
                        F.before(PLACE[earlier]) if past else F.now(PLACE[earlier])
                        if u in IN_TURN:
                            TO.now(9 if u in QK_A else 1)
                out = bank(u)
                if u in V_UNITS:
                    n = V_UNITS.index(u)
                    cols = bass.ds(pair * (2 * DH), 2 * DH)
                    for j in range(4):
                        rows = slice((n * 4 + j) * P, (n * 4 + j + 1) * P)
                        to = out[:, j * P:(j + 1) * P]
                        pe.matmul(to, xs_hi[:, rows], wv_hi[:, cols], start=True, stop=False)
                        pe.matmul(to, xs_lo[:, rows], wv_hi[:, cols], start=False, stop=False)
                        ins = pe.matmul(to, xs_hi[:, rows], wv_lo[:, cols], start=False, stop=True)
                elif u == TURN:
                    I.now(0)
                    ins = pe.transpose(out[0:SLOTS, 0:P], row_inv[:, :], k.ident[:, :])
                elif u in SCALE_UNITS:
                    n = SCALE_UNITS.index(u)
                    if n == 0:
                        F.now(PLACE[TURN])
                    for b in range(4):
                        ins = pe.matmul(out[:, b * P:(b + 1) * P], pick[:, n * 4 + b, :], scale[:, :],
                                        start=True, stop=True)
                elif u in OUT_UNITS:
                    n = OUT_UNITS.index(u)
                    F.now(PLACE[SCALE_UNITS[n]])
                    if n == 0:
                        WO.now(0)
                    ins = pe.matmul(out, wo_now[:, :], o_norm[:, n * HALF:(n + 1) * HALF], start=True, stop=True)
                else:
                    h, half = projection(u)
                    if u == QK_B[0]:
                        W.before(1)
                    if u == QK_A[0]:
                        W.before(0) if first else W.now(0)
                        pe.wait_ge(xs_in, xs_count)
                        pe.reg_add(xs_count, xs_count, 32)
                    at = slice(half * HALF, (half + 1) * HALF)
                    hi = w_hi[h][:, :, :].rearrange("p m d -> p (m d)")
                    lo = w_lo[h][:, :, :].rearrange("p m d -> p (m d)")
                    pe.matmul(out, hi, xs_hi[:, at], start=True, stop=False)
                    pe.matmul(out, hi, xs_lo[:, at], start=False, stop=False)
                    ins = pe.matmul(out, lo, xs_hi[:, at], start=False, stop=True)
                ins.then_inc(unit_ok, 1)

            def forward():
                for r in (E, TO, O, I, F, W, VC, WO, TW):
                    r.forward()

            W.fixed = 0
            pe.wait_ge(wv_ok, 1)
            for u in QK_A:
                one_unit(u, first=True)
            for r in (E, TO, O, I, F, W, VC, WO, TW):
                r.enter_loop()
            pe.wait_ge(primed, 12)
            pe.wait_ge(wo_in, 16)
            pe.wait_ge(consts, 3)
            with pe.Fori(0, ROUNDS) as it:
                for s in range(SLOTS):
                    if s in PLACE:
                        one_unit(s, it & (PAIRS - 1))
                    scores(s)
                    if s == TURN_SLOT:
                        one_unit(TURN)
                    turn_round(s)
                    if s in PV_AT:
                        product(s)
                forward()
            for r in (E, TO, O, I, F, VC, WO):
                r.leave_loop(ROUNDS)
            turn_round(0)
            turn_round(1)
            for s in (2, 3, 4, 5):
                product(s)
            F.before(UNITS - 1)
            F.leave_loop(ROUNDS, NOT_DONE)
            for u in (TURN, *SCALE_UNITS, *OUT_UNITS):
                one_unit(u, first=True)
            for g in range(GROUPS):
                if g == 0:
                    E.now(0)
                    F.now(PLACE[OUT_UNITS[1]])
                if g >= 4:
                    pe.wait_ge(x_ok, g - 3)
                for c in range(GROUP):
                    to = score[g // 2 % 2][:, g % 2 * HALF + c * P:g % 2 * HALF + (c + 1) * P]
                    ins = pe.transpose(to, yT[:, (g * GROUP + c) * P:(g * GROUP + c + 1) * P], k.ident[:, :])
                ins.then_inc(back_ok, 1)


def linear_attention(nc, k, wq_dram, wk_dram, wv_dram, wo_dram, wg_dram, bg_dram):
    HEADS, DH = 16, 8
    GATE_EPS, DEN_EPS = 1e-6, 1e-6
    HALVES = N // GT
    ROUNDS = B
    LEAD = 2
    COLS = DH + 1
    RING = 4
    WEIGHTS = 5
    WQ, WK, WG, WV, WO = range(WEIGHTS)
    ZQ, ZK, ZG = (slice(n * GT, (n + 1) * GT) for n in range(3))
    SUM_ORDER = [1, 2, 3, 0, 4, 5, 6, 7, 8]
    SUM_AT = {j: n for n, j in enumerate(SUM_ORDER)}

    with ExitStack() as stack:
        s_ = Scope(nc, stack, "linear")
        sb, ps, sem = s_.sb, s_.ps, s_.sem
        two = range(2)
        w = sb("w", [P, WEIGHTS, D])
        wT_hi, wT_lo = sb("wT_hi", [P, 3, D], F32R), sb("wT_lo", [P, 3, D], F32R)
        wv_hi, wv_lo = sb("wv_hi", [P, DH, HEADS, DH], F32R), sb("wv_lo", [P, DH, HEADS, DH], F32R)
        woT = sb("woT", [P, D])
        bg, ones = sb("bg", [P, 1]), sb("ones", [P, GT])
        same_head = sb("same_head", [P, HEADS, DH])
        into = sb("into", [P, DH, HEADS, DH])
        xs_hi = [sb(f"xs_hi{i}", [P, GT], F32R) for i in two]
        xs_lo = [sb(f"xs_lo{i}", [P, GT], F32R) for i in two]
        log = sb("log", [P, 2 * GT])
        gate, soft_q = sb("gate", [P, GT]), sb("soft_q", [P, GT])
        q, kk = ([sb(f"{n}{i}", [P, GT]) for i in two] for n in ("q", "k"))
        v_col = [sb(f"v_col{i}", [P, GT]) for i in two]
        kv_dve, kv_pool = ([sb(f"{n}{i}", [P, GT]) for i in two] for n in ("kv_dve", "kv_pool"))
        cum = [[sb(f"cum{i}_{j}", [P, GT]) for j in range(COLS)] for i in two]
        prod0 = [sb(f"prod0_{i}", [P, GT]) for i in two]
        prod = [sb(f"prod{i}", [P, GT]) for i in range(RING)]
        den_inv, oT = ([sb(f"{n}{i}", [P, GT]) for i in two] for n in ("den_inv", "oT"))
        z = ps("z", (P, 3 * GT))
        v_ps = [ps(f"v_ps{i}") for i in two]
        num = [ps(f"num{i}") for i in two]
        den_y = ps("den_y")

        w_in, bg_in, turned_ok, hi_ok, wT_ok, cleared, same_ok, const_ok = (sem(n) for n in (
            "w_in", "bg_in", "turned_ok", "hi_ok", "wT_ok", "cleared", "same_ok", "const_ok"))
        xs_in = [sem(f"xs_in{i}") for i in two]
        (z_ok, v_ok, v_out, kv_dve_ok, kv_pool_ok, cum_ok, prod_ok, sum_ok, gate_ok, log_step, soft_ok, q_ok,
         den_step, oT_ok, y_ok, x_ok) = (sem(n) for n in (
             "z_ok", "v_ok", "v_out", "kv_dve_ok", "kv_pool_ok", "cum_ok", "prod_ok", "sum_ok", "gate_ok", "log_step",
             "soft_ok", "q_ok", "den_step", "oT_ok", "y_ok", "x_ok"))
        PER = {id(x): n * HALVES for x, n in (
            (z_ok, 1), (v_ok, DH), (v_out, 4), (kv_dve_ok, 4), (kv_pool_ok, 4), (cum_ok, COLS), (prod_ok, COLS),
            (sum_ok, COLS), (gate_ok, 1), (log_step, 3), (soft_ok, 2), (q_ok, 1), (den_step, 2), (oT_ok, 1), (y_ok, 1), (x_ok, 1))}

        def rounds(engine, *sems):
            scratch = engine.alloc_register(f"linear_value_{engine.engine.name}")
            return [Rounds(engine, x, PER[id(x)], scratch) for x in sems]

        def at(r, g, n=0):
            m = g * (r.per // HALVES) + n
            r.now(m) if m >= 0 else r.before(m + r.per)

        def pipeline(slot, engine, sems):
            for x in sems:
                x.fixed = 0
            for n in range(LEAD):
                slot(n, 0)
            for x in sems:
                x.enter_loop()
            with engine.Fori(0, ROUNDS - 1) as r:
                for n in range(LEAD, LEAD + HALVES):
                    slot(n, r)
                for x in sems:
                    x.forward()
            for x in sems:
                x.fixed = (ROUNDS - 1) * x.per
            for n in range(LEAD, LEAD + HALVES):
                slot(n, ROUNDS - 1)

        def exists(g, r):
            return g >= 0 and not (isinstance(r, int) and r == ROUNDS - 1 and g >= HALVES)

        block = s_.block()

        @block.sync
        def _(sync):
            for n, d in enumerate((wq_dram, wk_dram, wg_dram, wv_dram, wo_dram)):
                sync.dma_start(w[:, n, :], d).then_inc(w_in, 16)
            sync.dma_start(bg[:, :], bg_dram.rearrange("(n a) -> n a", a=1)).then_inc(bg_in, 16)

            def fetch(g, i):
                sync.dma_start(f(xs_hi[i][:, :]), k.xT_hi[:, bass.ds(g * GT + i * GT, GT)]).then_inc(xs_in[i], 16)
                sync.dma_start(f(xs_lo[i][:, :]), k.xT_lo[:, bass.ds(g * GT + i * GT, GT)]).then_inc(xs_in[i], 16)
            V, = rounds(sync, v_ok)
            V.enter_loop()
            for i in two:
                fetch(0, i)
            with sync.Fori(1, ROUNDS) as r:
                for i in two:
                    at(V, i, DH - 1)
                    fetch(r * HALVES, i)
                V.forward()

        @block.gpsimd
        def _(pool):
            for x in (kv_pool_ok, prod_ok):
                pool.sem_inc(x, PER[id(x)])
            pool.memset(same_head[:, :, :], 1.0).then_inc(cleared, 1)
            pool.memset(into[:, :, :, :], 0.0).then_inc(cleared, 1)
            pool.memset(ones[:, :], 1.0).then_inc(const_ok, 1)
            pool.wait_ge(cleared, 2)
            pool.affine_select(out=same_head[:, :, :], in_=same_head[:, :, :], compare_op=ALU.is_ge, fill=0.0, base=0,
                               pattern=[[-DH, HEADS], [0, DH]], channel_multiplier=1).then_inc(same_ok, 1)
            pool.wait_ge(same_ok, 1)
            pool.affine_select(out=same_head[:, :, :], in_=same_head[:, :, :], compare_op=ALU.is_ge, fill=0.0,
                               base=DH - 1, pattern=[[DH, HEADS], [0, DH]], channel_multiplier=-1).then_inc(same_ok, 1)
            pool.wait_ge(same_ok, 2)
            for e in range(DH):
                pool.tensor_copy(into[:, e, :, e], same_head[:, :, e]).then_inc(const_ok, 1)
            V, C, S, SO, Q = waits = rounds(pool, v_out, cum_ok, sum_ok, soft_ok, q_ok)

            def slot(s, r):
                g = s - 1
                if not exists(g, r):
                    return
                i = g % 2

                def kv(j):
                    n = j // 2 - 1
                    if j == 2:
                        at(SO, g, 0)
                    at(V, g, n)
                    at(C, g, j - 4) if n >= 2 else at(C, g - 1, j + 4)
                    pool.tensor_tensor(kv_pool[n % 2][:, :], v_col[n % 2][:, :], kk[i][:, :], ALU.mult).then_inc(kv_pool_ok, 1)

                def product(j):
                    if j == 0:
                        at(Q, g)
                    at(C, g, j)
                    if j == 0:
                        at(S, g - 2, SUM_AT[0])
                    else:
                        at(S, g, SUM_AT[j - RING]) if j > RING else at(S, g - 1, SUM_AT[j + DH - RING])
                    out = prod0[i] if j == 0 else prod[(j - 1) % RING]
                    pool.tensor_tensor(out[:, :], q[i][:, :], cum[i][j][:, :], ALU.mult).then_inc(prod_ok, 1)

                kv(2)
                product(0)
                kv(4)
                product(1)
                product(2)
                kv(6)
                product(3)
                product(4)
                kv(8)
                for j in range(5, 9):
                    product(j)

            pipeline(slot, pool, waits)

        @block.scalar
        def _(act):
            for x in (v_out, gate_ok, log_step):
                act.sem_inc(x, PER[id(x)])
            act.wait_ge(turned_ok, 1)
            act.activation(wT_hi[:, :, :].rearrange("p a b -> p (a b)"), z[:, 0:3 * D], ACT.Copy).then_inc(hi_ok, 1)
            wvT = z[:, WV * D:(WV + 1) * D].rearrange("p (h e) -> p e h", h=HEADS).unsqueeze(3)
            act.activation(wv_hi[:, :, :, :], wvT.to_broadcast([P, DH, HEADS, DH]), ACT.Copy).then_inc(hi_ok, 1)
            act.activation(woT[:, :], z[:, WO * D:(WO + 1) * D], ACT.Copy).then_inc(hi_ok, 1)
            act.wait_ge(bg_in, 16)
            act.wait_ge(const_ok, 1 + DH)
            Z, V, L, SO, Q, KP = waits = rounds(act, z_ok, v_ok, log_step, soft_ok, q_ok, kv_pool_ok)

            def slot(s, r):
                g = s - 1

                def v_column(j):
                    if exists(g, r):
                        n = j // 2 - 1
                        at(V, g, j - 1)
                        at(KP, g, n - 2)
                        act.activation(v_col[n % 2][:, :], v_ps[j % 2][:, :], ACT.Copy).then_inc(v_out, 1)

                v_column(2)
                if exists(s, r):
                    at(Z, s)
                    at(Q, s - 1)
                    act.activation(gate[:, :], z[:, ZG], ACT.Sigmoid, bias=bg[:, :]).then_inc(gate_ok, 1)
                v_column(4)
                if exists(s, r):
                    at(SO, s - 1, 1)
                    act.activation(log[:, :], z[:, ZQ.start:ZK.stop], ACT.Abs).then_inc(log_step, 1)
                    at(L, s, 0)
                    act.activation(log[:, :], log[:, :], ACT.Exp, scale=-1.0).then_inc(log_step, 1)
                v_column(6)
                if exists(s, r):
                    at(L, s, 1)
                    act.activation(log[:, :], log[:, :], ACT.Ln, bias=ones[:, 0:1]).then_inc(log_step, 1)
                v_column(8)

            pipeline(slot, act, waits)

        @block.vector
        def _(dve):
            for x in (kv_dve_ok, cum_ok, soft_ok, q_ok, den_step, oT_ok, x_ok):
                dve.sem_inc(x, PER[id(x)])
            dve.wait_ge(hi_ok, 3)
            dve.tensor_tensor(wT_lo[:, :, :].rearrange("p a b -> p (a b)"), z[:, 0:3 * D],
                              f(wT_hi[:, :, :].rearrange("p a b -> p (a b)")), ALU.subtract).then_inc(wT_ok, 1)
            wvT = z[:, WV * D:(WV + 1) * D].rearrange("p (h e) -> p e h", h=HEADS).unsqueeze(3)
            dve.tensor_tensor(wv_lo[:, :, :, :], wvT.to_broadcast([P, DH, HEADS, DH]),
                              f(wv_hi[:, :, :, :]), ALU.subtract).then_inc(wT_ok, 1)
            dve.wait_ge(const_ok, 1 + DH)
            V, KD, KP, C, PR, SU, G, L, SO, DE, OT, Y = waits = rounds(
                dve, v_ok, kv_dve_ok, kv_pool_ok, cum_ok, prod_ok, sum_ok, gate_ok, log_step, soft_ok, den_step, oT_ok, y_ok)

            def slot(s, r):
                g, back = s - 1, s - 2
                i = g % 2

                def kv(j):
                    n = j // 2
                    if j == 1:
                        at(SO, g, 0)
                    at(V, g, j - 1)
                    at(C, g, j - 4) if n >= 2 else at(C, g - 1, j + 4)
                    dve.tensor_tensor(kv_dve[n % 2][:, :], v_ps[j % 2][:, :], kk[i][:, :], ALU.mult).then_inc(kv_dve_ok, 1)

                def scan(j):
                    if j == 0:
                        src = kk[i]
                    elif j % 2:
                        at(KD, g, j // 2)
                        src = kv_dve[j // 2 % 2]
                    else:
                        at(KP, g, j // 2 - 1)
                        src = kv_pool[(j // 2 - 1) % 2]
                    at(PR, g - 2, j)
                    at(C, g - 1, j)
                    start = cum[0][j][:, GT - 1:GT] if i else 0.0
                    dve.tensor_tensor_scan(cum[i][j][:, :], ones[:, :], src[:, :], start,
                                           ALU.mult, ALU.add).then_inc(cum_ok, 1)

                main, front, out = exists(g, r), exists(s, r), exists(back, r)
                if main:
                    kv(1)
                    scan(0)
                    kv(3)
                if out:
                    at(SU, back, COLS - 1)
                    at(DE, back, 1)
                    at(Y, back - 2)
                    dve.tensor_tensor(oT[back % 2][:, :], num[back % 2][:, :], den_inv[back % 2][:, :],
                                      ALU.mult).then_inc(oT_ok, 1)
                if main:
                    scan(1)
                    scan(2)
                    kv(5)
                if out:
                    at(Y, back)
                    x = k.x[:, bass.ds(r * (HALVES * GROUP) + back * GROUP, GROUP), :]
                    dve.tensor_tensor(x, den_y[:, :].rearrange("p (c d) -> p c d", d=D), x, ALU.add).then_inc(x_ok, 1)
                if main:
                    scan(3)
                    scan(4)
                    kv(7)
                    scan(5)
                    at(SU, g, SUM_AT[0])
                    at(OT, g - 2)
                    dve.tensor_scalar(den_inv[i][:, :], den_y[:, :], DEN_EPS, None, ALU.add).then_inc(den_step, 1)
                    scan(6)
                if front:
                    at(L, s, 2)
                    at(PR, s - 2, COLS - 1)
                    at(C, s - 2, 0)
                    dve.scalar_tensor_tensor(out=kk[s % 2][:, :], in0=z[:, ZK], scalar=0.0, in1=log[:, ZK],
                                             op0=ALU.max, op1=ALU.add).then_inc(soft_ok, 1)
                    dve.scalar_tensor_tensor(out=soft_q[:, :], in0=z[:, ZQ], scalar=0.0, in1=log[:, ZQ],
                                             op0=ALU.max, op1=ALU.add).then_inc(soft_ok, 1)
                if main:
                    scan(7)
                if front:
                    at(G, s)
                    at(SO, s, 1)
                    dve.scalar_tensor_tensor(out=q[s % 2][:, :], in0=gate[:, :], scalar=GATE_EPS, in1=soft_q[:, :],
                                             op0=ALU.add, op1=ALU.mult).then_inc(q_ok, 1)
                if main:
                    scan(8)
                    at(DE, g, 0)
                    dve.reciprocal(den_inv[i][:, :], den_inv[i][:, :]).then_inc(den_step, 1)

            pipeline(slot, dve, waits)

        @block.tensor
        def _(pe):
            for x in (z_ok, v_ok, sum_ok, y_ok):
                pe.sem_inc(x, PER[id(x)])
            pe.wait_ge(w_in, 16 * WEIGHTS)
            for n in range(WEIGHTS):
                ins = pe.transpose(z[:, n * D:(n + 1) * D], w[:, n, :], k.ident[:, :])
            ins.then_inc(turned_ok, 1)
            pe.wait_ge(wT_ok, 2)
            pe.wait_ge(const_ok, 1 + DH)
            KD, VO, PR, SO, G, OT, X, DE = waits = rounds(pe, kv_dve_ok, v_out, prod_ok, soft_ok, gate_ok, oT_ok, x_ok, den_step)
            xs_count, xs_value = pe.alloc_register("linear_xs_count"), pe.alloc_register("linear_xs_value")
            pe.reg_mov(xs_count, 0)

            def three(out, w_hi, w_lo, x_hi, x_lo):
                pe.matmul(out, w_hi, x_hi, start=True, stop=False)
                pe.matmul(out, w_hi, x_lo, start=False, stop=False)
                return pe.matmul(out, w_lo, x_hi, start=False, stop=True)

            def projections(g, r):
                i = g % 2
                if isinstance(r, int):
                    pe.wait_ge(xs_in[i], 32 * (r + g // 2 + 1))
                else:
                    pe.reg_add(xs_value, xs_count, 32 * (g // 2 + 1))
                    pe.wait_ge(xs_in[i], xs_value)
                at(SO, g - 1, 1)
                at(G, g - 1)
                for n, cols in ((WG, ZG), (WQ, ZQ), (WK, ZK)):
                    ins = three(z[:, cols], wT_hi[:, n, :], wT_lo[:, n, :], xs_hi[i][:, :], xs_lo[i][:, :])
                ins.then_inc(z_ok, 1)

            def v_column(g, j):
                if j % 2:
                    at(KD, g, j // 2 - 1)
                else:
                    at(VO, g, j // 2 - 2)
                hi, lo = (t[:, j - 1, :, :].rearrange("p h d -> p (h d)") for t in (wv_hi, wv_lo))
                three(v_ps[j % 2][:, :], hi, lo, xs_hi[g % 2][:, :], xs_lo[g % 2][:, :]).then_inc(v_ok, 1)

            def sum_over_d(g, j):
                at(PR, g, j)
                if j == 0:
                    at(X, g - 1)
                    pe.matmul(den_y[:, :], same_head[:, :, :].rearrange("p h d -> p (h d)"), prod0[g % 2][:, :],
                              start=True, stop=True).then_inc(sum_ok, 1)
                else:
                    if j == 1:
                        at(OT, g - 2)
                    pe.matmul(num[g % 2][:, :], into[:, j - 1, :, :].rearrange("p h d -> p (h d)"),
                              prod[(j - 1) % RING][:, :], start=(j == 1), stop=(j == DH)).then_inc(sum_ok, 1)

            def slot(s, r):
                g, back = s - 1, s - 2
                main, front, out = exists(g, r), exists(s, r), exists(back, r)
                if front:
                    projections(s, r)
                if main:
                    v_column(g, 3)
                    v_column(g, 4)
                if out:
                    at(OT, back)
                    at(DE, back, 0)
                    for c in range(GROUP):
                        at_c = slice(c * P, (c + 1) * P)
                        ins = pe.matmul(den_y[:, at_c], oT[back % 2][:, at_c], woT[:, :], start=True, stop=True)
                    ins.then_inc(y_ok, 1)
                if main:
                    v_column(g, 5)
                    sum_over_d(g, 1)
                    v_column(g, 6)
                    sum_over_d(g, 2)
                    v_column(g, 7)
                    sum_over_d(g, 3)
                    sum_over_d(g, 0)
                    v_column(g, 8)
                    sum_over_d(g, 4)
                if front:
                    v_column(s, 1)
                if main:
                    sum_over_d(g, 5)
                if front:
                    v_column(s, 2)
                if main:
                    sum_over_d(g, 6)
                    sum_over_d(g, 7)
                    sum_over_d(g, 8)
                if s == LEAD + HALVES - 1:
                    pe.reg_add(xs_count, xs_count, 32)

            pipeline(slot, pe, waits)


def store(nc, k, out_dram):
    with ExitStack() as stack:
        s = Scope(nc, stack, "store")
        stored = s.sem("stored")
        block = s.block()

        @block.sync
        def _(sync):
            for b in range(B):
                sync.dma_start(out_dram[b].rearrange("(c p) d -> p c d", p=P),
                               k.x[:, b * 8:(b + 1) * 8, :]).then_inc(stored, 16)
            sync.wait_ge(stored, 16 * B)


class Kept:
    pass


def network(nc, x, a_wq, a_wkv, a_wo, a_bo, b_wq, b_wk, b_wv, b_wo, b_wg, b_bg, router_w, expert_w, out):
    with ExitStack() as stack:
        s = Scope(nc, stack, "kept")
        k = Kept()
        k.x = s.sb("x", [P, CHUNKS, D])
        k.xT_hi, k.xT_lo = s.sb("xT_hi", [P, T]), s.sb("xT_lo", [P, T])
        k.ident = s.sb("ident", [P, P])
        k.eps = s.sb("eps", [P, 1])
        load_constants(nc, k, x)
        normalise(nc, k, "norm_a")
        attention(nc, k, a_wq, a_wkv, a_wo, a_bo)
        k.gate = s.sb("gate", [P, CHUNKS, expert_w.shape[0]])
        k.w_hi, k.w_lo = (s.sb(n, [P, expert_w.shape[0], D], F32R) for n in ("w_hi", "w_lo"))
        normalise(nc, k, "norm_f1", router_w, expert_w)
        experts(nc, k, "experts1")
        normalise(nc, k, "norm_b")
        linear_attention(nc, k, b_wq, b_wk, b_wv, b_wo, b_wg, b_bg)
        normalise(nc, k, "norm_f2", router_w)
        experts(nc, k, "experts2")
        store(nc, k, out)

_INS = ['L0_attn_a_x', 'L0_attn_a_Wq', 'L0_attn_a_Wkv', 'L0_attn_a_Wo', 'L0_attn_a_bo', 'L0_attn_b_Wq', 'L0_attn_b_Wk',
        'L0_attn_b_Wv', 'L0_attn_b_Wo', 'L0_attn_b_Wg', 'L0_attn_b_bg', 'L0_ffn_router_w', 'L0_ffn_expert_weights']
_OUTS = [((B, N, D), 'float32')]


def kernel(**inputs):
    import numpy as _np
    import concourse.bacc as _bacc
    from concourse import mybir as _mybir
    from concourse.bass_utils import run_bass_kernel_spmd as _run

    nc = _bacc.Bacc("TRN2", target_bir_lowering=False, num_devices=1)
    arrays, args = {}, []
    for name in _INS:
        a = _np.ascontiguousarray(inputs[name])
        arrays[f"in_{name}_dram"] = a
        args.append(nc.dram_tensor(f"in_{name}_dram", a.shape, _mybir.dt.from_np(a.dtype), kind="ExternalInput").ap())
    for i, (shape, dtype) in enumerate(_OUTS):
        dt = _mybir.dt.from_np(_np.dtype(dtype))
        args.append(nc.dram_tensor(f"out_{i}_dram", shape, dt, kind="ExternalOutput").ap())
    network(nc, *args)
    r = _run(nc, [arrays], core_ids=[0])
    got = tuple(r.results[0][f"out_{i}_dram"] for i in range(len(_OUTS)))
    return got[0]
```
